# Optimizing a Trainium2 kernel written in Bass

```python
import numpy as np
import jax
import jax.numpy as jnp

def _softmax(x, axis=-1):
    return jax.nn.softmax(x, axis=axis)

def _gelu(x):
    return jax.nn.gelu(x, approximate=True)

def _silu(x):
    return jax.nn.silu(x)

def _sigmoid(x):
    return jax.nn.sigmoid(x)

def _layernorm(x, axis=-1, eps=1e-05):
    m = jnp.mean(x, axis=axis, keepdims=True)
    v = jnp.var(x, axis=axis, keepdims=True)
    return (x - m) / jnp.sqrt(v + eps)

def _scatter_add(tgt, idx, src, axis=0):
    return tgt.at[idx].add(src)

def _segment_sum(src, seg, n):
    return jax.ops.segment_sum(src, seg, n)
kernel_name = 'mk_cond_seq_d2_seqx_r4_c9cc2d'

def setup_inputs(seed: int=0):
    np.random.seed(seed)
    _w = jnp.asarray

    def _rec_inputs():
        import jax
        import jax.numpy as jnp
        _rk = jax.random.key(seed)
        x = -0.0002928 + 1 * jax.random.normal(jax.random.fold_in(_rk, 1), (128, 64, 256), jnp.float32)
        _lenS = 64 - jax.random.randint(jax.random.fold_in(_rk, 7), (128,), 0, max(1, 64 // 4) + 1, jnp.int32)
        _lenS2 = 64 - jax.random.randint(jax.random.fold_in(_rk, 8), (128,), 0, max(1, 64 // 4) + 1, jnp.int32)
        itok_B_0_7 = jax.random.randint(jax.random.fold_in(_rk, 11), (128,), 0, 8, jnp.int32)
        itok_B_0_15 = jax.random.randint(jax.random.fold_in(_rk, 12), (128,), 0, 16, jnp.int32)
        return (x, itok_B_0_7, itok_B_0_15)
    x, itok_B_0_7, itok_B_0_15 = _rec_inputs()

    def _L0_cond_setup():
        import jax, jax.numpy as jnp
        import numpy as np
        E, H, I = (8, 256, 1024)
        B, S = (4, 256)
        LN_EPS = 1e-12
        key = jax.random.key(seed)
        ks = jax.random.split(key, 8)
        x = jax.random.normal(ks[0], (B, S, H), dtype=jnp.float32)
        expert_idx = jax.random.randint(ks[1], (B,), 0, E, dtype=jnp.int64)
        Wi = jax.random.normal(ks[2], (E, H, I), dtype=jnp.float32) * 0.02
        bi = jnp.zeros((E, I), dtype=jnp.float32)
        Wo = jax.random.normal(ks[3], (E, I, H), dtype=jnp.float32) * 0.02
        bo = jnp.zeros((E, H), dtype=jnp.float32)
        gamma = jnp.ones((E, H), dtype=jnp.float32)
        beta = jnp.zeros((E, H), dtype=jnp.float32)
        return {'input_tensor': x, 'expert_idx': expert_idx, 'Wi': Wi, 'bi': bi, 'Wo': Wo, 'bo': bo, 'gamma': gamma, 'beta': beta}
    _L0_cond_all = _L0_cond_setup()
    _L0_cond_in = {k: v for k, v in _L0_cond_all.items() if k in ('Wi', 'bi', 'Wo', 'bo', 'gamma', 'beta')}
    del _L0_cond_all

    def _L1_cond_setup():
        import jax, jax.numpy as jnp
        import numpy as np
        B, S, D = (32, 256, 256)
        A = 64
        E = 16
        LN_EPS = 1e-05
        key = jax.random.key(seed)
        ks = jax.random.split(key, 10)
        s = lambda fan_in: 1.0 / np.sqrt(fan_in)
        return {'hidden_states': jax.random.normal(ks[0], (B, S, D), dtype=jnp.float32), 'domain_id': jax.random.randint(ks[1], (B,), 0, E, dtype=jnp.int64), 'down_W': jax.random.uniform(ks[2], (A, D), jnp.float32, -s(D), s(D)), 'down_b': jax.random.uniform(ks[3], (A,), jnp.float32, -s(D), s(D)), 'up_W': jax.random.uniform(ks[4], (D, A), jnp.float32, -s(A), s(A)), 'up_b': jax.random.uniform(ks[5], (D,), jnp.float32, -s(A), s(A)), 'expert_W': jax.random.uniform(ks[6], (E, A, A), jnp.float32, -s(A), s(A)), 'expert_b': jax.random.uniform(ks[7], (E, A), jnp.float32, -s(A), s(A)), 'domain_emb': jax.random.normal(ks[8], (E, A), dtype=jnp.float32), 'ln_gamma': jnp.ones((D,), jnp.float32), 'ln_beta': jnp.zeros((D,), jnp.float32)}
    _L1_cond_all = _L1_cond_setup()
    _L1_cond_in = {k: v for k, v in _L1_cond_all.items() if k in ('down_W', 'down_b', 'up_W', 'up_b', 'expert_W', 'expert_b', 'domain_emb', 'ln_gamma', 'ln_beta')}
    del _L1_cond_all
    return {'x': x, 'itok_B_0_7': itok_B_0_7, 'itok_B_0_15': itok_B_0_15, 'L0_cond_Wi': _L0_cond_in['Wi'], 'L0_cond_bi': _L0_cond_in['bi'], 'L0_cond_Wo': _L0_cond_in['Wo'], 'L0_cond_bo': _L0_cond_in['bo'], 'L0_cond_gamma': _L0_cond_in['gamma'], 'L0_cond_beta': _L0_cond_in['beta'], 'L1_cond_down_W': _L1_cond_in['down_W'], 'L1_cond_down_b': _L1_cond_in['down_b'], 'L1_cond_up_W': _L1_cond_in['up_W'], 'L1_cond_up_b': _L1_cond_in['up_b'], 'L1_cond_expert_W': _L1_cond_in['expert_W'], 'L1_cond_expert_b': _L1_cond_in['expert_b'], 'L1_cond_domain_emb': _L1_cond_in['domain_emb'], 'L1_cond_ln_gamma': _L1_cond_in['ln_gamma'], 'L1_cond_ln_beta': _L1_cond_in['ln_beta']}

def reference(x, itok_B_0_7, itok_B_0_15, L0_cond_Wi, L0_cond_bi, L0_cond_Wo, L0_cond_bo, L0_cond_gamma, L0_cond_beta, L1_cond_down_W, L1_cond_down_b, L1_cond_up_W, L1_cond_up_b, L1_cond_expert_W, L1_cond_expert_b, L1_cond_domain_emb, L1_cond_ln_gamma, L1_cond_ln_beta):
    import jax
    import jax.numpy as jnp

    def _L0_cond_ref(input_tensor, expert_idx, Wi, bi, Wo, bo, gamma, beta):
        import jax, jax.numpy as jnp
        import numpy as np
        E, H, I = (8, 256, 1024)
        B, S = (4, 256)
        LN_EPS = 1e-12
        Wi_b = Wi[expert_idx]
        bi_b = bi[expert_idx]
        Wo_b = Wo[expert_idx]
        bo_b = bo[expert_idx]
        g_b = gamma[expert_idx]
        be_b = beta[expert_idx]
        h = jax.nn.gelu(jnp.einsum('bsh,bhi->bsi', input_tensor, Wi_b) + bi_b[:, None, :], approximate=False)
        o = jnp.einsum('bsi,bih->bsh', h, Wo_b) + bo_b[:, None, :]
        r = o + input_tensor
        mu = jnp.mean(r, axis=-1, keepdims=True)
        var = jnp.mean(jnp.square(r - mu), axis=-1, keepdims=True)
        y = (r - mu) * jax.lax.rsqrt(var + LN_EPS)
        return y * g_b[:, None, :] + be_b[:, None, :]

    def _L1_cond_ref(hidden_states, domain_id, down_W, down_b, up_W, up_b, expert_W, expert_b, domain_emb, ln_gamma, ln_beta):
        import jax, jax.numpy as jnp
        import numpy as np
        B, S, D = (32, 256, 256)
        A = 64
        E = 16
        LN_EPS = 1e-05
        residual = hidden_states
        hidden = jnp.einsum('bsd,ad->bsa', hidden_states, down_W) + down_b
        hidden = jax.nn.gelu(hidden, approximate=False)
        valid = (domain_id >= 0) & (domain_id < E)
        idx = jnp.clip(domain_id, 0, E - 1)
        Wsel = expert_W[idx]
        bsel = expert_b[idx]
        expert_out = jnp.einsum('bsa,boa->bso', hidden, Wsel) + bsel[:, None, :]
        domain_output = jnp.where(valid[:, None, None], expert_out, hidden)
        hidden = domain_output + domain_emb[idx][:, None, :]
        hidden = jnp.einsum('bsa,da->bsd', hidden, up_W) + up_b
        x = hidden + residual
        mu = jnp.mean(x, axis=-1, keepdims=True)
        var = jnp.mean(jnp.square(x - mu), axis=-1, keepdims=True)
        return (x - mu) * jax.lax.rsqrt(var + LN_EPS) * ln_gamma + ln_beta
    x = _L0_cond_ref(x, itok_B_0_7, L0_cond_Wi, L0_cond_bi, L0_cond_Wo, L0_cond_bo, L0_cond_gamma, L0_cond_beta)
    x = _L1_cond_ref(x, itok_B_0_15, L1_cond_down_W, L1_cond_down_b, L1_cond_up_W, L1_cond_up_b, L1_cond_expert_W, L1_cond_expert_b, L1_cond_domain_emb, L1_cond_ln_gamma, L1_cond_ln_beta)
    return x

_drawn_inputs = setup_inputs


def setup_inputs(seed=0):
    import zlib

    import numpy as np

    out = dict(_drawn_inputs(seed))
    spreads = {'L0_cond_bi': (0.0, 0.1),
     'L0_cond_bo': (0.0, 0.1),
     'L0_cond_gamma': (1.0, 0.2),
     'L0_cond_beta': (0.0, 0.1),
     'L1_cond_ln_gamma': (1.0, 0.2),
     'L1_cond_ln_beta': (0.0, 0.1)}
    factors = {'L1_cond_down_b': 8.0}
    for name, (base, spread) in spreads.items():
        noise = np.random.default_rng([zlib.crc32(name.encode()), seed]).standard_normal(out[name].shape)
        drawn = base * np.exp(spread * noise) if base else spread * noise
        out[name] = jnp.asarray(drawn.astype(out[name].dtype))
    for name, factor in factors.items():
        out[name] = (out[name] * factor).astype(out[name].dtype)
    return out
```

```python
import concourse.bass as bass
from concourse import mybir
from contextlib import ExitStack

B, S, D = 128, 64, 256
E0, I = 8, 1024
E1, A = 16, 64
P = 128
KD, KI = D // P, I // P
TILES = B // 2 + E0 // 2
SLOTS = 2 * TILES
ENTRIES = E1 + 2
WCH, NCH = 512, 8
CHUNKS = E0 * NCH
QC = WCH // 2
FIRST_CHUNKS = 10
STAGES = 6
XS, HS, WS = 8.0, 8.0, 512.0
EPS0, EPS1 = 1e-12, 1e-5
LEAD = 6
STEPS = TILES + 3

IDX_SRC, IDX_DST, IDX_DOM = 0, SLOTS, 2 * SLOTS
IDX_POS = 3 * SLOTS
IDX_EXP = IDX_POS + TILES
IDX_CHUNK = IDX_EXP + TILES
IDX_LEN = IDX_CHUNK + CHUNKS


def build(nc, t):
    fp32, f16, i32 = mybir.dt.float32, mybir.dt.float16, mybir.dt.int32
    ALU, ACT, AX = mybir.AluOpType, mybir.ActivationFunctionType, mybir.AxisListType

    ctx = ExitStack()
    with ctx:
        def sb(name, shape, dt=fp32):
            return ctx.enter_context(nc.sbuf_tensor(name, shape, dt))

        def pb(name, shape):
            return ctx.enter_context(nc.psum_tensor(name, shape, fp32))

        def sem(name):
            return ctx.enter_context(nc.semaphore(name))

        W = [sb(f"W{c}", [P, E0, 2, 2, QC], f16) for c in range(NCH)]
        w_flat = [w[:, :, :, :, :].rearrange("p e u r q -> p (e u r q)") for w in W]
        PLACE = 2 * WCH
        stage = sb("stage", [P, STAGES, WCH])
        bo_t = sb("bo_t", [P, E0 * D])
        g_t = sb("g_t", [P, E0 * D])
        be_t = sb("be_t", [P, E0 * D])
        bi_c = sb("bi_c", [P, E0 * KI])
        gb_c = sb("gb_c", [P, E0 * 2 * KD])
        lng = sb("lng", [P, D])
        lnb = sb("lnb", [P, D])
        upb = sb("upb", [P, D])
        upT = sb("upT", [P, D])
        downT = sb("downT", [P, KD, 2, A])
        downb = sb("downb", [P, 1])
        ada = sb("ada", [P, ENTRIES, A + 1])
        emb = sb("emb", [P, E1])
        ident = sb("ident", [P, P])

        x_nat = sb("x_nat", [P, 2, D])
        x_T = sb("x_T", [P, 2, KD, P])
        x_hi = sb("x_hi", [P, 2, KD, P], f16)
        x_lo = sb("x_lo", [P, 2, KD, P], f16)
        x_bo = sb("x_bo", [P, 2, D])
        bi_tile = sb("bi_tile", [P, 2, KI])
        h = sb("h", [P, KI, P])
        h_hi = sb("h_hi", [P, 2, KI, P], f16)
        h_lo = sb("h_lo", [P, 2, KI, P], f16)
        r1 = sb("r1", [P, D])
        st1 = sb("st1", [P, 6])
        mv1 = sb("mv1", [P, 2])
        ve1 = sb("ve1", [P, 1])
        rs1 = sb("rs1", [P, 1])
        z1 = sb("z1", [P, D])
        gb_tile = sb("gb_tile", [P, 2 * KD])
        yT = sb("yT", [P, KD, P])
        y_up = sb("y_up", [P, 2, D])
        a1 = sb("a1", [P, S])
        ada_tile = sb("ada_tile", [P, 2, A + 1])
        a2 = sb("a2", [P, P])
        r2 = sb("r2", [P, D])
        st2 = sb("st2", [P, 6])
        mv2 = sb("mv2", [P, 2])
        ve2 = sb("ve2", [P, 1])
        rs2 = sb("rs2", [P, 1])
        z2 = sb("z2", [P, D])
        y = sb("y", [P, 2, D])
        neg_half = sb("neg_half", [P, 1])
        eps = sb("eps", [P, 3])

        taken = {"h": 0, "x_bo": 0}
        homes = {"h": h[:, :, :].rearrange("p c q -> p (c q)"), "x_bo": x_bo[:, :, :].rearrange("p c q -> p (c q)")}

        def early(*shape, home="h"):
            n = shape[0] if len(shape) == 1 else shape[0] * shape[1]
            a = homes[home][:, taken[home]:taken[home] + n]
            taken[home] += n
            return a if len(shape) == 1 else a.rearrange("p (a b) -> p a b", b=shape[1])

        iota_r = early(SLOTS)
        at_slot = early(SLOTS)
        before = early(SLOTS)
        below = early(P)
        ones = early(P)
        lower_e = early(E0, E0)
        ahead = early(E0, E0)
        same = early(E0, E0)
        cube = h_hi[0:1, :, :, :].rearrange("p a c q -> p (a c q)").bitcast(fp32)[:, 0:TILES * E0]\
            .rearrange("p (t e) -> p t e", e=E0)
        row = h_lo[0:1, :, :, :].rearrange("p a c q -> p (a c q)").bitcast(fp32)[:, 0:4 * SLOTS]\
            .rearrange("p (t e) -> p t e", e=SLOTS)
        tok_i = sb("tok_i", [P, 2], i32)
        tok = sb("tok", [P, 2])
        tmp = sb("tmp", [P, 4])
        iota_p = sb("iota_p", [P, 3])
        iota_e = early(E0, home="x_bo")
        exb = early(E1, home="x_bo")
        onehot = early(E0, home="x_bo")
        pairs_i = sb("pairs_i", [P, E0], i32)
        pairs_h = sb("pairs_h", [P, E0], i32)
        pairs = early(E0, home="x_bo")
        place = early(E0, home="x_bo")
        first = early(E0, home="x_bo")
        last = early(E0, home="x_bo")
        where = early(E0, home="x_bo")
        slot = sb("slot", [P, 1])
        pos_f = early(TILES)[0:1]
        exp_f = early(TILES)[0:1]
        ord_f = early(E0, home="x_bo")[0:1]
        chunk_f = early(E0, NCH, home="x_bo")[0:1]
        idx = sb("idx", [1, IDX_LEN], i32)

        p_h = [pb(f"p_h{n}", [P, KI, P]) for n in range(2)]
        p_o = pb("p_o", [P, 512])
        p_t = pb("p_t", [P, 512])
        p_d = pb("p_d", [P, 512])
        p_u = pb("p_u", [P, 512])

        tok_in = sem("tok_in")
        tables_in = sem("tables_in")
        ada_in = sem("ada_in")
        w_in = [sem(f"w_in{n}") for n in range(STAGES)]
        xnat_in = [sem(f"xnat_in{n}") for n in range(2)]
        xT_in = [sem(f"xT_in{n}") for n in range(2)]
        y_out = [sem(f"y_out{n}") for n in range(2)]
        iota_ready = sem("iota_ready")
        const_ready = sem("const_ready")
        sort_step = sem("sort_step")
        pool_step = sem("pool_step")
        counts_ready = sem("counts_ready")
        slots_ready = sem("slots_ready")
        rows_ready = sem("rows_ready")
        idx_ready = sem("idx_ready")
        ada_ready = sem("ada_ready")
        tables_ready = sem("tables_ready")
        w_first_hi = sem("w_first_hi")
        w_first = sem("w_first")
        w_hi = sem("w_hi")
        w_lo = sem("w_lo")
        xhi_done = sem("xhi_done")
        x_split = sem("x_split")
        xbo_done = sem("xbo_done")
        bi_done = sem("bi_done")
        s1_half = sem("s1_half")
        s1_done = s1_half
        gelu_half = sem("gelu_half")
        hhi_half = sem("hhi_half")
        hlo_half = sem("hlo_half")
        s2_done = sem("s2_done")
        r1_part = sem("r1_part")
        r1_done = sem("r1_done")
        st1_done = sem("st1_done")
        mv1_done = sem("mv1_done")
        ve1_done = sem("ve1_done")
        rs1_done = sem("rs1_done")
        z1_done = sem("z1_done")
        tr_done = sem("tr_done")
        gb_done = sem("gb_done")
        yT_done = sem("yT_done")
        yg_done = sem("yg_done")
        yup_part = sem("yup_part")
        yup_done = sem("yup_done")
        down_done = sem("down_done")
        a1_done = sem("a1_done")
        ada_done = sem("ada_done")
        exp_done = sem("exp_done")
        a2_done = sem("a2_done")
        up_done = sem("up_done")
        r2_done = sem("r2_done")
        st2_done = sem("st2_done")
        mv2_done = sem("mv2_done")
        ve2_done = sem("ve2_done")
        rs2_done = sem("rs2_done")
        z2_done = sem("z2_done")
        zg_done = sem("zg_done")
        y_done = sem("y_done")

        block = ctx.enter_context(nc.Block())

        def need(eng, s, value):
            if isinstance(value, int) and value <= 0:
                return
            eng.wait_ge(s, value)

        def index(eng, at, top):
            return nc.values_load(idx[0:1, bass.ds(at, 1)], engines=[eng.engine], min_val=0, max_val=top,
                                  skip_runtime_bounds_check_because="the sorting clips every index")

        HALF = [slice(0, A), slice(A, 2 * A)]
        MAT = [slice(1, A + 1), slice(0, A)]
        COL = [slice(0, 1), slice(A, A + 1)]

        def tile_ok(n, i):
            return not isinstance(i, int) or 0 <= i < TILES

        def run(eng, step, unroll=2):
            for i in range(LEAD):
                step(i, i % 2, ((i + FIRST_CHUNKS) % NCH, (i + FIRST_CHUNKS) // NCH))
            mid = CHUNKS - FIRST_CHUNKS
            for begin, end, weights, times in ((LEAD, mid, True, unroll), (mid, TILES - 2, False, 2)):
                with eng.Fori(0, (end - begin) // times) as n:
                    i = eng.snap(n * times + begin)
                    for q in range(times):
                        step(i + q, q % 2, (q, n + (FIRST_CHUNKS + begin) // NCH) if weights else False)
            for i in range(TILES - 2, STEPS):
                step(i, i % 2, False)

        def loads(i, parity, each):
            n = 16 * each
            return ((i - parity) // 2 + 1) * n if isinstance(i, int) else (i - parity) * (n // 2) + n

        def w_loads(i, parity):
            early = len([m for m in range(FIRST_CHUNKS) if m % STAGES == parity])
            if isinstance(i, int):
                return 16 * (early + i // 2 + 1)
            return (i - parity) * 8 + 16 * (early + 1)

        @block.sync
        def _(sp):
            sp.dma_start(tok_i[:, 0:1], t["itok0"].rearrange("(p a) -> p a", a=1)).then_inc(tok_in, 16)
            sp.dma_start(tok_i[:, 1:2], t["itok1"].rearrange("(p a) -> p a", a=1)).then_inc(tok_in, 16)
            sp.dma_start(bi_c[:, :], t["bi"]).then_inc(tables_in, 16)
            sp.dma_start(gb_c[:, :], t["gb"]).then_inc(tables_in, 16)
            for n in range(2):
                half = HALF[n]
                sp.dma_start(ada[half, 0:E1, MAT[n]], t["expert_W"]).then_inc(ada_in, 16)
                sp.dma_start(exb[half, :], t["expert_b"]).then_inc(ada_in, 16)
                sp.dma_start(emb[half, :], t["emb"]).then_inc(ada_in, 16)
            sp.wait_ge(idx_ready, 1)

            def load_chunk(m, slot_n):
                c = index(sp, IDX_CHUNK + m, CHUNKS - 1)
                sp.dma_start(stage[:, slot_n, :], t["w"][bass.ds(c * P, P), :]).then_inc(w_in[slot_n], 16)

            def load_tile(i, parity):
                for n in range(2):
                    b = index(sp, 2 * i + (IDX_SRC + n), B - 1)
                    sp.dma_start(x_T[:, parity, :, S * n:S * n + S],
                                 t["xT"][bass.ds(b * P, P), :].rearrange("p (k s) -> p k s", k=KD))\
                      .then_inc(xT_in[parity], 16)
                    sp.dma_start(x_nat[S * n:S * n + S, parity, :], t["x"][bass.ds(b * S, S), :])\
                      .then_inc(xnat_in[parity], 16)

            load_chunk(0, 0)
            load_tile(0, 0)
            for m in range(1, STAGES):
                load_chunk(m, m)
            load_tile(1, 1)
            sp.dma_start(bo_t[:, :], t["bo"].partition_broadcast(P)).then_inc(tables_in, 16)
            sp.dma_start(g_t[:, :], t["gamma"].partition_broadcast(P)).then_inc(tables_in, 16)
            for m in range(STAGES, FIRST_CHUNKS):
                sp.wait_ge(w_first, m - STAGES + 1)
                load_chunk(m, m % STAGES)
            sp.dma_start(be_t[:, :], t["beta"].partition_broadcast(P)).then_inc(tables_in, 16)
            for dst, name in ((upb, "up_b"), (lng, "ln_gamma"), (lnb, "ln_beta")):
                sp.dma_start(dst[:, :], t[name].partition_broadcast(P)).then_inc(tables_in, 16)
            for n in range(2):
                half = HALF[n]
                sp.dma_start(upT[half, :], t["up_W"]).then_inc(tables_in, 16)
                sp.dma_start(downb[half, :], t["down_b"].rearrange("(p a) -> p a", a=1)).then_inc(tables_in, 16)
                for k in range(KD):
                    sp.dma_start(downT[:, k, n, :], t["down_W"][k * P:k * P + P, :]).then_inc(tables_in, 16)

            def step(i, parity, weights):
                if weights:
                    if isinstance(i, int) and i < 2:
                        sp.wait_ge(w_first, i + STAGES + 1)
                    else:
                        sp.wait_ge(w_lo, i - 1)
                    load_chunk(i + FIRST_CHUNKS, parity)
                if tile_ok(0, i + 2) and not (isinstance(i, int) and i + 2 >= TILES):
                    need(sp, x_split, i + 1)
                    need(sp, xbo_done, i + 1)
                    load_tile(i + 2, parity)
                if tile_ok(0, i - 3):
                    need(sp, y_done, i - 2)
                    for n in range(2):
                        b = index(sp, 2 * i + (IDX_DST + n - 6), SLOTS - 1)
                        sp.dma_start(t["out"][bass.ds(b * S, S), :], y[S * n:S * n + S, 1 - parity, :])\
                          .then_inc(y_out[1 - parity], 16)

            run(sp, step)
            for n in range(2):
                sp.wait_ge(y_out[n], 16 * TILES)

        @block.gpsimd
        def _(pool):
            pool.iota(iota_p[:, 0:1], [[0, 1]], base=0, channel_multiplier=1, allow_small_or_imprecise_dtypes=True).then_inc(iota_ready, 1)
            pool.iota(iota_r[:, :], [[1, SLOTS]], base=0, channel_multiplier=0, allow_small_or_imprecise_dtypes=True).then_inc(iota_ready, 1)
            pool.iota(iota_e[:, :], [[1, E0]], base=0, channel_multiplier=0, allow_small_or_imprecise_dtypes=True).then_inc(iota_ready, 1)
            pool.memset(iota_p[:, 1:2], 1.0).then_inc(iota_ready, 1)
            pool.memset(ones[:, :], 1.0).then_inc(iota_ready, 1)
            pool.iota(below[:, :], [[1, P]], base=0, channel_multiplier=-1, allow_small_or_imprecise_dtypes=True).then_inc(iota_ready, 1)
            pool.iota(lower_e[:, :, :], [[1, E0], [-1, E0]], base=0, channel_multiplier=0, allow_small_or_imprecise_dtypes=True).then_inc(iota_ready, 1)
            pool.memset(neg_half[:, :], -0.5).then_inc(const_ready, 1)
            pool.memset(eps[:, 0:1], EPS0).then_inc(const_ready, 1)
            pool.memset(eps[:, 1:2], EPS1).then_inc(const_ready, 1)
            pool.memset(eps[:, 2:3], WS).then_inc(const_ready, 1)
            pool.memset(ada_tile[:, :, :], 0.0).then_inc(const_ready, 1)
            pool.memset(a2[:, :], 0.0).then_inc(const_ready, 1)
            n_pool = [0]

            def link(ins):
                n_pool[0] += 1
                ins.then_inc(pool_step, 1)
                pool.wait_ge(pool_step, n_pool[0])

            pool.wait_ge(iota_ready, 7)
            pool.wait_ge(const_ready, 6)
            link(pool.memset(ada[:, E1:ENTRIES, :], 0.0))
            for n in range(2):
                for e in range(E1, ENTRIES):
                    eye = ada[HALF[n], e, MAT[n]]
                    link(pool.affine_select(out=eye, in_=eye, compare_op=ALU.not_equal, fill=1.0, base=0,
                                            pattern=[[-1, A]], channel_multiplier=1))
            pool.wait_ge(ada_in, 6 * 16)
            for n in range(2):
                col = ada[HALF[n], :, COL[n]].rearrange("p e a -> p (e a)")
                link(pool.tensor_copy(col[:, E1:E1 + 1], emb[HALF[n], 0:1]))
                link(pool.tensor_copy(col[:, E1 + 1:E1 + 2], emb[HALF[n], E1 - 1:E1]))
                link(pool.tensor_tensor(col[:, 0:E1], exb[HALF[n], :], emb[HALF[n], :], ALU.add))
            pool.sem_inc(ada_ready, 1)
            pool.wait_ge(idx_ready, 1)
            pool.wait_ge(tables_in, 2 * 16)

            def gather_bi(i, parity):
                e = index(pool, i + IDX_EXP, E0 - 1)
                need(pool, gelu_half, 2 * i - 2)
                pool.tensor_copy(bi_tile[:, parity, :], bi_c[:, bass.ds(e * KI, KI)]).then_inc(bi_done, 1)

            gather_bi(0, 0)
            pool.wait_ge(tables_in, 16 * 16)
            for e in range(E0):
                pool.tensor_tensor(be_t[:, e * D:e * D + D], be_t[:, e * D:e * D + D], upb[:, :], ALU.add)\
                    .then_inc(tables_ready, 1)
            pool.wait_ge(tables_ready, E0)

            def step(i, parity, weights):
                if tile_ok(0, i - 2):
                    e = index(pool, i + (IDX_EXP - 2), E0 - 1)
                    need(pool, yT_done, i - 2)
                    pool.tensor_copy(gb_tile[:, :], gb_c[:, bass.ds(e * 2 * KD, 2 * KD)]).then_inc(gb_done, 1)
                    pool.wait_ge(mv1_done, i - 1)
                    pool.tensor_tensor(ve1[:, :], mv1[:, 1:2], eps[:, 0:1], ALU.add).then_inc(ve1_done, 1)
                    pool.wait_ge(ve1_done, i - 1)
                    pool.tensor_tensor(rs1[:, :], ve1[:, :], neg_half[:, :], ALU.pow).then_inc(rs1_done, 1)
                if tile_ok(0, i - 3):
                    pool.wait_ge(mv2_done, i - 2)
                    pool.tensor_tensor(ve2[:, :], mv2[:, 1:2], eps[:, 1:2], ALU.add).then_inc(ve2_done, 1)
                    pool.wait_ge(ve2_done, i - 2)
                    pool.tensor_tensor(rs2[:, :], ve2[:, :], neg_half[:, :], ALU.pow).then_inc(rs2_done, 1)
                if tile_ok(0, i - 2):
                    pool.wait_ge(z1_done, i - 1)
                    pool.tensor_tensor(y_up[:, parity, :], z1[:, :], g_t[:, bass.ds(e * D, D)], ALU.mult)\
                        .then_inc(yg_done, 1)
                    pool.wait_ge(yg_done, i - 1)
                    pool.tensor_tensor(y_up[:, parity, :], y_up[:, parity, :], be_t[:, bass.ds(e * D, D)], ALU.add)\
                        .then_inc(yup_done, 1)
                if tile_ok(0, i - 3):
                    pool.wait_ge(z2_done, i - 2)
                    if not isinstance(i, int) or i >= 5:
                        pool.wait_ge(y_out[1 - parity], loads(i - 5, 1 - parity, 2))
                    pool.tensor_tensor(y[:, 1 - parity, :], z2[:, :], lng[:, :], ALU.mult).then_inc(zg_done, 1)
                    pool.wait_ge(zg_done, i - 2)
                    pool.tensor_tensor(y[:, 1 - parity, :], y[:, 1 - parity, :], lnb[:, :], ALU.add).then_inc(y_done, 1)
                if tile_ok(0, i):
                    e = index(pool, i + IDX_EXP, E0 - 1)
                    pool.wait_ge(xnat_in[parity], loads(i, parity, 2))
                    pool.tensor_tensor(x_bo[:, parity, :], x_nat[:, parity, :], bo_t[:, bass.ds(e * D, D)],
                                       ALU.add).then_inc(xbo_done, 1)
                if tile_ok(0, i + 1):
                    gather_bi(i + 1, 1 - parity)

            run(pool, step)

        @block.scalar
        def _(act):
            def chunk_high(c, place_n, slot_n):
                return nc.scalar.activation(W[c][:, bass.ds(place_n, 1), :, 0, :],
                                            stage[:, slot_n, :].rearrange("p (a u q) -> p a u q", a=1, u=2),
                                            ACT.Copy, scale=WS)

            for m in range(FIRST_CHUNKS):
                act.wait_ge(w_in[m % STAGES], 16 * (m // STAGES + 1))
                chunk_high(m % NCH, m // NCH, m % STAGES).then_inc(w_first_hi, 1)

            def gelu(i, parity, half):
                if half == 0:
                    act.wait_ge(bi_done, i + 1)
                act.wait_ge(s1_half, 2 * i + (half + 1))
                need(act, hlo_half, 2 * i + (half - 1))
                for c in range(half * KI // 2, (half + 1) * KI // 2):
                    ins = nc.scalar.activation(h[:, c, :], p_h[parity][:, c, :], ACT.Gelu,
                                               bias=bi_tile[:, parity, c:c + 1], scale=1.0 / (XS * WS))
                ins.then_inc(gelu_half, 1)

            def high_h(i, parity, half):
                cols = slice(half * KI // 2, (half + 1) * KI // 2)
                act.wait_ge(gelu_half, 2 * i + (half + 1))
                nc.scalar.activation(h_hi[:, parity, cols, :], h[:, cols, :], ACT.Copy, scale=HS).then_inc(hhi_half, 1)

            def step(i, parity, weights):
                if tile_ok(0, i - 2):
                    need(act, a2_done, 2 * i - 4)
                    for n in range(2):
                        d = index(act, 2 * i + (IDX_DOM + n - 4), ENTRIES - 1)
                        nc.scalar.copy(ada_tile[HALF[n], n, :], ada[HALF[n], bass.ds(d, 1), :]).then_inc(ada_done, 1)
                if tile_ok(0, i):
                    gelu(i, parity, 0)
                    high_h(i, parity, 0)
                if tile_ok(0, i - 2):
                    act.wait_ge(tr_done, i - 1)
                    act.wait_ge(gb_done, i - 1)
                    for k in range(KD):
                        ins = nc.scalar.activation(yT[:, k, :], p_t[:, k * P:k * P + P], ACT.Identity,
                                                   bias=gb_tile[:, KD + k:KD + k + 1], scale=gb_tile[:, k:k + 1])
                    ins.then_inc(yT_done, 1)
                if tile_ok(0, i):
                    gelu(i, parity, 1)
                    high_h(i, parity, 1)
                if tile_ok(0, i - 2):
                    act.wait_ge(down_done, i - 1)
                    for n in range(2):
                        half = HALF[n]
                        nc.scalar.activation(a1[half, :], p_d[half, S * n:S * n + S], ACT.Gelu,
                                             bias=downb[half, :]).then_inc(a1_done, 1)
                if weights:
                    act.wait_ge(w_in[parity], w_loads(i, parity))
                    chunk_high(*weights, parity).then_inc(w_hi, 1)

            act.wait_ge(ada_ready, 1)
            act.wait_ge(tables_in, 16 * 16)
            run(act, step, NCH)

        @block.vector
        def _(dve):
            n_sort = [0]

            def link(ins):
                n_sort[0] += 1
                ins.then_inc(sort_step, 1)
                dve.wait_ge(sort_step, n_sort[0])

            v = nc.vector

            def wide(a):
                return a.unsqueeze(2).to_broadcast([a.shape[0], a.shape[1], E0])

            def rows(a, n):
                return a.unsqueeze(1).to_broadcast([a.shape[0], n, a.shape[1]])

            dve.wait_ge(tok_in, 32)
            dve.wait_ge(iota_ready, 7)
            link(v.tensor_copy(tok[:, :], tok_i[:, :]))
            link(v.tensor_scalar(tmp[:, 0:1], tok[:, 0:1], 0.0, float(E0), ALU.is_lt, ALU.mult))
            link(v.tensor_tensor(tmp[:, 1:2], tok[:, 0:1], tmp[:, 0:1], ALU.add))
            link(v.tensor_scalar(tok[:, 0:1], tmp[:, 1:2], 0.0, float(E0 - 1), ALU.max, ALU.min))
            link(v.tensor_scalar(tmp[:, 2:3], tok[:, 1:2], -1.0, float(E1), ALU.max, ALU.min))
            link(v.tensor_scalar(tmp[:, 0:1], tmp[:, 2:3], 0.0, float(E1 + 1), ALU.is_lt, ALU.mult))
            link(v.tensor_scalar(tmp[:, 1:2], tmp[:, 2:3], float(E1), None, ALU.is_ge))
            link(v.tensor_tensor(tmp[:, 3:4], tmp[:, 2:3], tmp[:, 0:1], ALU.add))
            link(v.tensor_tensor(iota_p[:, 2:3], tmp[:, 3:4], tmp[:, 1:2], ALU.add))
            link(v.tensor_scalar(ident[:, :], below[:, :], 0.0, None, ALU.is_equal))
            link(v.tensor_scalar(below[:, :], below[:, :], 0.0, None, ALU.is_gt))
            link(v.tensor_scalar(lower_e[:, :, :], lower_e[:, :, :], 0.0, None, ALU.is_gt))
            v.tensor_scalar(onehot[:, :], iota_e[:, :], tok[:, 0:1], None, ALU.is_equal).then_inc(counts_ready, 1)
            dve.wait_ge(counts_ready, 2)
            link(v.tensor_scalar(pairs_i[:, :], p_o[:, E0:2 * E0], 1.0, None, ALU.add))
            link(v.tensor_scalar(pairs_h[:, :], pairs_i[:, :], 1, None, ALU.logical_shift_right))
            link(v.tensor_copy(pairs[:, :], pairs_h[:, :]))
            link(v.tensor_tensor(ahead[:, :, :], rows(pairs[:, :], E0), wide(pairs[:, :]), ALU.is_gt))
            link(v.tensor_tensor(same[:, :, :], rows(pairs[:, :], E0), wide(pairs[:, :]), ALU.is_equal))
            link(v.tensor_tensor(same[:, :, :], same[:, :, :], lower_e[:, :, :], ALU.mult))
            link(v.tensor_tensor(ahead[:, :, :], ahead[:, :, :], same[:, :, :], ALU.add))
            link(v.tensor_reduce(place[:, :], ahead[:, :, :], AX.X, ALU.add))
            link(v.tensor_tensor(same[:, :, :], ahead[:, :, :], rows(pairs[:, :], E0), ALU.mult))
            link(v.tensor_reduce(first[:, :], same[:, :, :], AX.X, ALU.add))
            link(v.tensor_tensor(last[:, :], first[:, :], pairs[:, :], ALU.add))
            link(v.scalar_tensor_tensor(where[:, :], first[:, :], 2.0, p_o[:, 0:E0], ALU.mult, ALU.add))
            link(v.tensor_tensor(where[:, :], where[:, :], onehot[:, :], ALU.mult))
            link(v.tensor_reduce(slot[:, :], where[:, :], AX.X, ALU.add))
            link(v.tensor_scalar(at_slot[:, :], iota_r[:, :], slot[:, :], None, ALU.is_equal))
            v.tensor_scalar(before[:, :], iota_r[:, :], slot[:, :], None, ALU.is_gt).then_inc(slots_ready, 1)
            link(v.tensor_tensor(cube[:, 0:E0, :], rows(place[0:1, :], E0), wide(iota_r[0:1, 0:E0]), ALU.is_equal))
            link(v.tensor_tensor(cube[:, 0:E0, :], cube[:, 0:E0, :], rows(iota_e[0:1, :], E0), ALU.mult))
            link(v.tensor_reduce(ord_f[:, :], cube[:, 0:E0, :], AX.X, ALU.add))
            link(v.scalar_tensor_tensor(chunk_f[:, :, :], wide(ord_f[:, :]), float(NCH), rows(iota_e[0:1, :], E0),
                                        ALU.mult, ALU.add))
            link(v.tensor_copy(idx[:, IDX_CHUNK:IDX_LEN], chunk_f[:, :, :].rearrange("a e c -> a (e c)")))
            link(v.tensor_tensor(cube[:, :, :], rows(last[0:1, :], TILES), wide(iota_r[0:1, 0:TILES]), ALU.is_le))
            link(v.tensor_reduce(pos_f[:, :], cube[:, :, :], AX.X, ALU.add))
            link(v.tensor_scalar(pos_f[:, :], pos_f[:, :], float(E0 - 1), None, ALU.min))
            link(v.tensor_scalar(idx[:, IDX_POS:IDX_EXP], pos_f[:, :], float(PLACE), None, ALU.mult))
            link(v.tensor_tensor(cube[:, :, :], rows(place[0:1, :], TILES), wide(pos_f[:, :]), ALU.is_equal))
            link(v.tensor_tensor(cube[:, :, :], cube[:, :, :], rows(iota_e[0:1, :], TILES), ALU.mult))
            link(v.tensor_reduce(exp_f[:, :], cube[:, :, :], AX.X, ALU.add))
            link(v.tensor_copy(idx[:, IDX_EXP:IDX_CHUNK], exp_f[:, :]))
            dve.wait_ge(rows_ready, 1)
            link(v.tensor_copy(idx[:, IDX_SRC:IDX_DST], p_t[0:1, 0:SLOTS]))
            link(v.tensor_copy(idx[:, IDX_DOM:IDX_POS], p_d[0:1, 0:SLOTS]))
            link(v.tensor_tensor(row[:, 0, :], iota_r[0:1, :], p_u[0:1, 0:SLOTS], ALU.subtract))
            link(v.tensor_scalar(row[:, 1, :], p_o[0:1, 0:SLOTS], -1.0, 1.0, ALU.mult, ALU.add))
            link(v.scalar_tensor_tensor(row[:, 2, :], row[:, 0, :], float(B), row[:, 1, :], ALU.add, ALU.mult))
            link(v.tensor_tensor(row[:, 3, :], row[:, 2, :], p_t[0:1, 0:SLOTS], ALU.add))
            v.tensor_copy(idx[:, IDX_DST:IDX_DOM], row[:, 3, :]).then_inc(idx_ready, 1)

            def high_x(i, parity):
                dve.wait_ge(xT_in[parity], loads(i, parity, 2))
                v.tensor_scalar(x_hi[:, parity, :, :], x_T[:, parity, :, :], XS, None, ALU.mult).then_inc(xhi_done, 1)

            def low_x(i, parity):
                dve.wait_ge(xhi_done, i + 1)
                v.scalar_tensor_tensor(x_lo[:, parity, :, :], x_T[:, parity, :, :], XS, x_hi[:, parity, :, :],
                                       ALU.mult, ALU.subtract).then_inc(x_split, 1)

            def chunk_low(c, place_n, slot_n):
                return v.scalar_tensor_tensor(W[c][:, bass.ds(place_n, 1), :, 1, :],
                                              stage[:, slot_n, :].rearrange("p (a u q) -> p a u q", a=1, u=2),
                                              WS, W[c][:, bass.ds(place_n, 1), :, 0, :], ALU.mult, ALU.subtract)

            for m in range(FIRST_CHUNKS):
                dve.wait_ge(w_first_hi, m + 1)
                chunk_low(m % NCH, m // NCH, m % STAGES).then_inc(w_first, 1)
                if m == 0:
                    high_x(0, 0)
                    low_x(0, 0)

            def split_h(i, parity, half):
                cols = slice(half * KI // 2, (half + 1) * KI // 2)
                dve.wait_ge(hhi_half, 2 * i + (half + 1))
                v.scalar_tensor_tensor(h_lo[:, parity, cols, :], h[:, cols, :], HS, h_hi[:, parity, cols, :],
                                       ALU.mult, ALU.subtract).then_inc(hlo_half, 1)

            def step(i, parity, weights):
                if tile_ok(0, i - 2):
                    dve.wait_ge(s2_done, i - 1)
                    dve.wait_ge(xbo_done, i - 1)
                    v.scalar_tensor_tensor(r1[:, :], p_o[:, 0:D], 1.0 / (HS * WS), x_bo[:, parity, :],
                                           ALU.mult, ALU.add).then_inc(r1_part, 1)
                    dve.wait_ge(r1_part, i - 1)
                    v.scalar_tensor_tensor(r1[:, :], p_o[:, D:2 * D], 1.0 / (HS * WS), r1[:, :],
                                           ALU.mult, ALU.add).then_inc(r1_done, 1)
                    dve.wait_ge(r1_done, i - 1)
                    v.bn_stats(st1[:, :], r1[:, :]).then_inc(st1_done, 1)
                if tile_ok(0, i - 2):
                    dve.wait_ge(st1_done, i - 1)
                if tile_ok(0, i + 1):
                    high_x(i + 1, 1 - parity)
                if tile_ok(0, i - 2):
                    v.bn_aggr(mv1[:, :], st1[:, :]).then_inc(mv1_done, 1)
                if tile_ok(0, i + 1):
                    low_x(i + 1, 1 - parity)
                if tile_ok(0, i - 3):
                    dve.wait_ge(up_done, i - 2)
                    dve.wait_ge(yup_done, i - 2)
                    v.tensor_tensor(r2[:, :], p_u[:, 0:D], y_up[:, 1 - parity, :], ALU.add).then_inc(r2_done, 1)
                    dve.wait_ge(r2_done, i - 2)
                    v.bn_stats(st2[:, :], r2[:, :]).then_inc(st2_done, 1)
                if tile_ok(0, i - 2):
                    dve.wait_ge(rs1_done, i - 1)
                    need(dve, st2_done, i - 2)
                    v.tensor_scalar(z1[:, :], r1[:, :], mv1[:, 0:1], rs1[:, :], ALU.subtract, ALU.mult)\
                        .then_inc(z1_done, 1)
                if tile_ok(0, i - 3):
                    if isinstance(i, int):
                        dve.wait_ge(st2_done, i - 2)
                    v.bn_aggr(mv2[:, :], st2[:, :]).then_inc(mv2_done, 1)
                if tile_ok(0, i):
                    split_h(i, parity, 0)
                if tile_ok(0, i - 3):
                    dve.wait_ge(rs2_done, i - 2)
                    v.tensor_scalar(z2[:, :], r2[:, :], mv2[:, 0:1], rs2[:, :], ALU.subtract, ALU.mult)\
                        .then_inc(z2_done, 1)
                if tile_ok(0, i):
                    split_h(i, parity, 1)
                if tile_ok(0, i - 2):
                    dve.wait_ge(exp_done, i - 1)
                    for n in range(2):
                        half = HALF[n]
                        v.tensor_scalar(a2[half, S * n:S * n + S], p_d[half, P:P + S], ada_tile[half, n, COL[n]],
                                        None, ALU.add).then_inc(a2_done, 1)
                if weights:
                    dve.wait_ge(w_hi, i + 1)
                    chunk_low(*weights, parity).then_inc(w_lo, 1)

            run(dve, step, NCH)

        @block.tensor
        def _(pe):
            mm = nc.tensor.matmul
            BATCH = 2
            pe.wait_ge(counts_ready, 1)
            pe.wait_ge(iota_ready, 7)
            mm(p_o[:, 0:E0], below[:, :], onehot[:, :], start=True, stop=True)
            mm(p_o[:, E0:2 * E0], ones[:, :], onehot[:, :], start=True, stop=True).then_inc(counts_ready, 1)
            pe.wait_ge(slots_ready, 1)
            mm(p_t[0:1, 0:SLOTS], iota_p[:, 0:1], at_slot[:, :], start=True, stop=True)
            mm(p_o[0:1, 0:SLOTS], iota_p[:, 1:2], at_slot[:, :], start=True, stop=True)
            mm(p_d[0:1, 0:SLOTS], iota_p[:, 2:3], at_slot[:, :], start=True, stop=True)
            mm(p_u[0:1, 0:SLOTS], iota_p[:, 1:2], before[:, :], start=True, stop=True).then_inc(rows_ready, 1)
            pe.wait_ge(idx_ready, 1)
            pe.wait_ge(const_ready, 6)

            def first_weights(place_reg, c, k):
                chunk, at = w_flat[k * 2 + c // 4], c % 4 // 2 * WCH + c % 2 * P
                return chunk[:, bass.ds(place_reg + at, P)], chunk[:, bass.ds(place_reg + (at + QC), P)]

            def second_weights(place_reg, j):
                chunk, at = w_flat[NCH // 2 + j // 2], j % 2 * WCH
                return chunk[:, bass.ds(place_reg + at, 2 * D)], chunk[:, bass.ds(place_reg + at, D)]

            def first_addresses(place_reg, cs):
                for k in range(KD):
                    for c in cs:
                        for part in first_weights(place_reg, c, k):
                            pe.lower_ap(part, for_matmul_weights=True)

            def second_addresses(place_reg, js):
                for j in js:
                    pe.lower_ap(second_weights(place_reg, j)[0])

            def first_product(parity, place_reg, c):
                for k in range(KD):
                    hi, lo = first_weights(place_reg, c, k)
                    mm(p_h[parity][:, c, :], hi, x_hi[:, parity, k, :], start=(k == 0), stop=False)
                    mm(p_h[parity][:, c, :], hi, x_lo[:, parity, k, :], start=False, stop=False)
                    ins = mm(p_h[parity][:, c, :], lo, x_hi[:, parity, k, :], start=False, stop=(k == KD - 1))
                return ins

            def second_product(parity, place_reg, j):
                both, hi = second_weights(place_reg, j)
                mm(p_o[:, :], h_hi[:, parity, j, :], both, start=(j == 0), stop=(j == KI - 1))
                return mm(p_o[:, 0:D], h_lo[:, parity, j, :], hi, start=False, stop=False, skip_group_check=True)

            def step(i, parity, weights):
                def up():
                    pe.wait_ge(a2_done, 2 * i - 4)
                    mm(p_u[:, 0:D], a2[:, :], upT[:, :], start=True, stop=True).then_inc(up_done, 1)

                def transpose():
                    pe.wait_ge(z1_done, i - 1)
                    for k in range(KD):
                        ins = nc.tensor.transpose(p_t[:, k * P:k * P + P], z1[:, k * P:k * P + P], ident[:, :])
                    ins.then_inc(tr_done, 1)

                if tile_ok(0, i):
                    here = index(pe, i + IDX_POS, (E0 - 1) * PLACE)
                    pe.wait_ge(x_split, i + 1)
                    if isinstance(i, int) and i < 2:
                        pe.wait_ge(w_first, NCH if i == 0 else FIRST_CHUNKS)
                    if weights:
                        need(pe, w_lo, i - (FIRST_CHUNKS - NCH))
                    else:
                        pe.wait_ge(w_lo, CHUNKS - FIRST_CHUNKS)
                    for c in range(KI):
                        if c % BATCH == 0:
                            first_addresses(here, range(c, c + BATCH))
                        ins = first_product(parity, here, c)
                        if c % (KI // 2) == KI // 2 - 1:
                            ins.then_inc(s1_half, 1)
                        if c == 1 and tile_ok(0, i - 3):
                            up()
                        if c == 5 and tile_ok(0, i - 2):
                            transpose()
                else:
                    if tile_ok(0, i - 3):
                        up()
                    if tile_ok(0, i - 2):
                        transpose()
                if tile_ok(0, i - 1):
                    there = index(pe, i + (IDX_POS - 1), (E0 - 1) * PLACE)
                    second_addresses(there, range(KI))
                    pe.wait_ge(hlo_half, 2 * i)
                    for j in range(KI // 2):
                        second_product(1 - parity, there, j)
                if tile_ok(0, i - 2):
                    pe.wait_ge(yT_done, i - 1)
                    for k in range(KD):
                        ins = mm(p_d[:, 0:P], downT[:, k, :, :], yT[:, k, :], start=(k == 0), stop=(k == KD - 1))
                    ins.then_inc(down_done, 1)
                if tile_ok(0, i - 1):
                    for j in range(KI // 2, KI):
                        ins = second_product(1 - parity, there, j)
                    ins.then_inc(s2_done, 1)
                if tile_ok(0, i - 2):
                    pe.wait_ge(a1_done, 2 * i - 2)
                    mm(p_d[:, P:P + S], ada_tile[:, :, :].rearrange("p n a -> p (n a)")[:, 1:2 * A + 1], a1[:, :], start=True, stop=True).then_inc(exp_done, 1)

            pe.wait_ge(tables_in, 16 * 16)
            run(pe, step)


def kernel(x, itok_B_0_7, itok_B_0_15, L0_cond_Wi, L0_cond_bi, L0_cond_Wo, L0_cond_bo, L0_cond_gamma,
           L0_cond_beta, L1_cond_down_W, L1_cond_down_b, L1_cond_up_W, L1_cond_up_b, L1_cond_expert_W,
           L1_cond_expert_b, L1_cond_domain_emb, L1_cond_ln_gamma, L1_cond_ln_beta):
    import numpy as np
    import concourse.bacc as bacc
    from concourse.bass_utils import run_bass_kernel_spmd

    wi = np.asarray(L0_cond_Wi).reshape(E0, KD, P, I // WCH, WCH).transpose(0, 1, 3, 2, 4)
    wo = np.asarray(L0_cond_Wo).reshape(E0, NCH // 2, WCH // D, P, D).transpose(0, 1, 3, 2, 4)
    w = np.concatenate([wi.reshape(E0, NCH // 2, P, WCH), wo.reshape(E0, NCH // 2, P, WCH)], axis=1)
    g = np.asarray(L0_cond_gamma).reshape(E0, KD, P).transpose(2, 0, 1)
    be = np.asarray(L0_cond_beta).reshape(E0, KD, P).transpose(2, 0, 1)
    arrays = {
        "itok0": itok_B_0_7,
        "itok1": itok_B_0_15,
        "x": np.asarray(x).reshape(B * S, D),
        "xT": np.asarray(x).reshape(B, S, KD, P).transpose(0, 3, 2, 1).reshape(B * P, KD * S),
        "w": w.reshape(CHUNKS * P, WCH),
        "bi": np.asarray(L0_cond_bi).reshape(E0, KI, P).transpose(2, 0, 1).reshape(P, E0 * KI),
        "gb": np.concatenate([g, be], axis=2).reshape(P, E0 * 2 * KD),
        "bo": np.asarray(L0_cond_bo).reshape(E0 * D),
        "gamma": np.asarray(L0_cond_gamma).reshape(E0 * D),
        "beta": np.asarray(L0_cond_beta).reshape(E0 * D),
        "down_W": np.asarray(L1_cond_down_W).T,
        "down_b": L1_cond_down_b,
        "up_W": np.asarray(L1_cond_up_W).T,
        "up_b": L1_cond_up_b,
        "expert_W": np.asarray(L1_cond_expert_W).transpose(2, 0, 1),
        "expert_b": np.asarray(L1_cond_expert_b).T,
        "emb": np.asarray(L1_cond_domain_emb).T,
        "ln_gamma": L1_cond_ln_gamma,
        "ln_beta": L1_cond_ln_beta,
    }
    nc = bacc.Bacc("TRN2", target_bir_lowering=False, num_devices=1)
    fed, t = {}, {}
    for name, a in arrays.items():
        a = np.ascontiguousarray(a)
        fed[f"in_{name}"] = a
        t[name] = nc.dram_tensor(f"in_{name}", a.shape, mybir.dt.from_np(a.dtype), kind="ExternalInput").ap()
    t["out"] = nc.dram_tensor("out", (SLOTS * S, D), mybir.dt.float32, kind="ExternalOutput").ap()
    build(nc, t)
    got = run_bass_kernel_spmd(nc, [fed], core_ids=[0]).results[0]["out"]
    return got.reshape(SLOTS, S, D)[:B]
```

```python
import concourse.bass as bass
from concourse import mybir
from contextlib import ExitStack

B, S, D = 128, 64, 256
E0, I = 8, 1024
E1, A = 16, 64
P = 128
KD, KI = D // P, I // P
TILES = B // 2 + E0 // 2
SLOTS = 2 * TILES
ENTRIES = E1 + 2
WCH, NCH = 512, 8
CHUNKS = E0 * NCH
QC = WCH // 2
FIRST_CHUNKS = NCH
STAGES = 6
SLOTS_W = 4
XS, HS, WS = 8.0, 8.0, 512.0
EPS0, EPS1 = 1e-12, 1e-5
LEAD = NCH
STEPS = TILES + 4

IDX_SRC, IDX_DST, IDX_DOM = 0, SLOTS, 2 * SLOTS
IDX_POS = 3 * SLOTS
IDX_EXP = IDX_POS + TILES
IDX_CHUNK = IDX_EXP + TILES
IDX_LEN = IDX_CHUNK + CHUNKS


def build(nc, t):
    fp32, f16, i32 = mybir.dt.float32, mybir.dt.float16, mybir.dt.int32
    ALU, ACT, AX = mybir.AluOpType, mybir.ActivationFunctionType, mybir.AxisListType

    ctx = ExitStack()
    with ctx:
        def sb(name, shape, dt=fp32):
            return ctx.enter_context(nc.sbuf_tensor(name, shape, dt))

        def pb(name, shape):
            return ctx.enter_context(nc.psum_tensor(name, shape, fp32))

        def sem(name):
            return ctx.enter_context(nc.semaphore(name))

        W = [sb(f"W{c}", [P, E0, 2, 2, QC], f16) for c in range(NCH)]
        w_flat = [w[:, :, :, :, :].rearrange("p e u r q -> p (e u r q)") for w in W]
        PLACE = 2 * WCH
        stage = sb("stage", [P, STAGES, WCH])
        bo_t = sb("bo_t", [P, E0 * D])
        g_t = sb("g_t", [P, E0 * D])
        be_t = sb("be_t", [P, E0 * D])
        bi_c = sb("bi_c", [P, E0 * KI])
        gb_c = sb("gb_c", [P, E0 * 2 * KD])
        lng = sb("lng", [P, D])
        lnb = sb("lnb", [P, D])
        upb = sb("upb", [P, D])
        upT = sb("upT", [P, D])
        downT = sb("downT", [P, KD, 2, A])
        downb = sb("downb", [P, 1])
        ada = sb("ada", [P, ENTRIES, A + 1])
        emb = sb("emb", [P, E1])
        ident = sb("ident", [P, P])

        x_nat = sb("x_nat", [P, 2, D])
        x_T = sb("x_T", [P, 2, KD, P])
        x_hi = sb("x_hi", [P, 2, KD, P], f16)
        x_lo = sb("x_lo", [P, 2, KD, P], f16)
        x_bo = sb("x_bo", [P, 2, D])
        bi_tile = sb("bi_tile", [P, 2, KI])
        h = sb("h", [P, KI, P])
        h_hi = sb("h_hi", [P, 2, KI, P], f16)
        h_lo = sb("h_lo", [P, 2, KI, P], f16)
        r1 = sb("r1", [P, D])
        st1 = sb("st1", [P, 6])
        mv1 = sb("mv1", [P, 2])
        ve1 = sb("ve1", [P, 1])
        rs1 = sb("rs1", [P, 1])
        z1 = sb("z1", [P, D])
        gb_tile = sb("gb_tile", [P, 2 * KD])
        yT = sb("yT", [P, KD, P])
        y_up = sb("y_up", [P, 2, D])
        a1 = sb("a1", [P, S])
        ada_tile = sb("ada_tile", [P, 2, A + 1])
        a2 = sb("a2", [P, P])
        r2 = sb("r2", [P, D])
        st2 = sb("st2", [P, 6])
        mv2 = sb("mv2", [P, 2])
        ve2 = sb("ve2", [P, 1])
        rs2 = sb("rs2", [P, 1])
        z2 = sb("z2", [P, D])
        y = sb("y", [P, 2, D])
        neg_half = sb("neg_half", [P, 2])
        eps = sb("eps", [P, 2])

        taken = {"h": 0, "x_bo": 0}
        homes = {"h": h[:, :, :].rearrange("p c q -> p (c q)"), "x_bo": x_bo[:, :, :].rearrange("p c q -> p (c q)")}

        def early(*shape, home="h"):
            n = shape[0] if len(shape) == 1 else shape[0] * shape[1]
            a = homes[home][:, taken[home]:taken[home] + n]
            taken[home] += n
            return a if len(shape) == 1 else a.rearrange("p (a b) -> p a b", b=shape[1])

        iota_r = early(SLOTS)
        at_slot = early(SLOTS)
        before = early(SLOTS)
        below = early(P)
        ones = early(P)
        lower_e = early(E0, E0)
        ahead = early(E0, E0)
        same = early(E0, E0)
        cube = h_hi[0:1, :, :, :].rearrange("p a c q -> p (a c q)").bitcast(fp32)[:, 0:TILES * E0]\
            .rearrange("p (t e) -> p t e", e=E0)
        row = h_lo[0:1, :, :, :].rearrange("p a c q -> p (a c q)").bitcast(fp32)[:, 0:4 * SLOTS]\
            .rearrange("p (t e) -> p t e", e=SLOTS)
        tok_i = sb("tok_i", [P, 2], i32)
        tok = sb("tok", [P, 2])
        tmp = sb("tmp", [P, 4])
        iota_p = sb("iota_p", [P, 3])
        iota_e = early(E0, home="x_bo")
        exb = early(E1, home="x_bo")
        onehot = early(E0, home="x_bo")
        pairs_i = sb("pairs_i", [P, E0], i32)
        pairs_h = sb("pairs_h", [P, E0], i32)
        pairs = early(E0, home="x_bo")
        place = early(E0, home="x_bo")
        first = early(E0, home="x_bo")
        last = early(E0, home="x_bo")
        where = early(E0, home="x_bo")
        slot = sb("slot", [P, 1])
        pos_f = early(TILES)[0:1]
        exp_f = early(TILES)[0:1]
        ord_f = early(E0, home="x_bo")[0:1]
        chunk_f = early(E0, NCH, home="x_bo")[0:1]
        idx = sb("idx", [1, IDX_LEN], i32)

        p_h = [pb(f"p_h{n}", [P, KI, P]) for n in range(2)]
        p_o = pb("p_o", [P, 512])
        p_t = pb("p_t", [P, 512])
        p_d = pb("p_d", [P, 512])
        p_u = pb("p_u", [P, 512])

        tok_in = sem("tok_in")
        cols_in = sem("cols_in")
        bo_in = sem("bo_in")
        adapter_in = sem("adapter_in")
        tables_in = sem("tables_in")
        ada_in = sem("ada_in")
        w_in = [sem(f"w_in{n}") for n in range(STAGES)]
        xnat_in = [sem(f"xnat_in{n}") for n in range(2)]
        xT_in = [sem(f"xT_in{n}") for n in range(2)]
        y_out = [sem(f"y_out{n}") for n in range(2)]
        CHUNK_READY, SRC_READY, TILE_READY, ALL_READY = 1, 2, 3, 4
        iota_ready = sem("iota_ready")
        const_ready = sem("const_ready")
        sort_step = sem("sort_step")
        pool_step = sem("pool_step")
        counts_ready = sem("counts_ready")
        slots_ready = sem("slots_ready")
        rows_ready = sem("rows_ready")
        idx_ready = sem("idx_ready")
        ada_ready = sem("ada_ready")
        tables_ready = sem("tables_ready")
        w_first_hi = sem("w_first_hi")
        w_first = sem("w_first")
        w_hi = sem("w_hi")
        w_lo = sem("w_lo")
        xhi_done = sem("xhi_done")
        x_split = sem("x_split")
        xbo_done = sem("xbo_done")
        bi_done = sem("bi_done")
        s1_half = sem("s1_half")
        s1_done = s1_half
        gelu_half = sem("gelu_half")
        hhi_half = sem("hhi_half")
        hlo_half = sem("hlo_half")
        s2_done = sem("s2_done")
        r1_part = sem("r1_part")
        r1_done = sem("r1_done")
        st1_done = sem("st1_done")
        mv1_done = sem("mv1_done")
        ve1_done = sem("ve1_done")
        rs1_done = sem("rs1_done")
        z1_done = sem("z1_done")
        tr_done = sem("tr_done")
        gb_done = sem("gb_done")
        yT_done = sem("yT_done")
        yg_done = sem("yg_done")
        yup_part = sem("yup_part")
        yup_done = sem("yup_done")
        down_done = sem("down_done")
        a1_done = sem("a1_done")
        ada_done = sem("ada_done")
        exp_done = sem("exp_done")
        a2_done = sem("a2_done")
        up_done = sem("up_done")
        r2_done = sem("r2_done")
        st2_done = sem("st2_done")
        mv2_done = sem("mv2_done")
        ve2_done = sem("ve2_done")
        rs2_done = sem("rs2_done")
        z2_done = sem("z2_done")
        zg_done = sem("zg_done")
        y_done = sem("y_done")

        block = ctx.enter_context(nc.Block())

        def need(eng, s, value):
            if isinstance(value, int) and value <= 0:
                return
            eng.wait_ge(s, value)

        def index(eng, at, top):
            return nc.values_load(idx[0:1, bass.ds(at, 1)], engines=[eng.engine], min_val=0, max_val=top,
                                  skip_runtime_bounds_check_because="the sorting clips every index")

        HALF = [slice(0, A), slice(A, 2 * A)]
        MAT = [slice(1, A + 1), slice(0, A)]
        COL = [slice(0, 1), slice(A, A + 1)]

        def tile_ok(n, i):
            return not isinstance(i, int) or 0 <= i < TILES

        def run(eng, step, unroll=2, ahead=0):
            lead, mid = LEAD - ahead, CHUNKS - FIRST_CHUNKS - ahead
            for i in range(lead):
                j = i + ahead
                step(i, i % 2, (j % NCH, (j + FIRST_CHUNKS) // NCH, j % SLOTS_W))
            for begin, end, weights, times in ((lead, mid, True, unroll), (mid, TILES - 2, False, 2)):
                with eng.Fori(0, (end - begin) // times) as n:
                    i = eng.snap(n * times + begin)
                    for q in range(times):
                        step(i + q, q % 2, (q, n + (FIRST_CHUNKS + LEAD) // NCH, (LEAD + q) % SLOTS_W)
                             if weights else False)
            for i in range(TILES - 2, STEPS):
                step(i, i % 2, False)

        def loads(i, parity, each):
            n = 16 * each
            return ((i - parity) // 2 + 1) * n if isinstance(i, int) else (i - parity) * (n // 2) + n

        def w_loads(i, slot_n):
            early = len([m for m in range(FIRST_CHUNKS) if m % STAGES == slot_n])
            return 16 * (early + i // SLOTS_W + 1) if isinstance(i, int) else (i - slot_n) * (16 // SLOTS_W) + 16 * (early + 1)

        @block.sync
        def _(sp):
            AHEAD = 2
            sp.dma_start(tok_i[:, 0:1], t["itok0"].rearrange("(p a) -> p a", a=1)).then_inc(tok_in, 16)
            sp.dma_start(tok_i[:, 1:2], t["itok1"].rearrange("(p a) -> p a", a=1)).then_inc(tok_in, 16)
            sp.dma_start(bi_c[:, :], t["bi"]).then_inc(cols_in, 16)
            sp.dma_start(gb_c[:, :], t["gb"]).then_inc(cols_in, 16)
            for n in range(2):
                half = HALF[n]
                sp.dma_start(ada[half, 0:E1, MAT[n]], t["expert_W"]).then_inc(ada_in, 16)
                sp.dma_start(exb[half, :], t["expert_b"]).then_inc(ada_in, 16)
                sp.dma_start(emb[half, :], t["emb"]).then_inc(ada_in, 16)
            sp.dma_start(bo_t[:, :], t["bo"].partition_broadcast(P)).then_inc(bo_in, 16)
            for n in range(2):
                half = HALF[n]
                for k in range(KD):
                    sp.dma_start(downT[:, k, n, :], t["down_W"][k * P:k * P + P, :]).then_inc(adapter_in, 16)
                sp.dma_start(downb[half, :], t["down_b"].rearrange("(p a) -> p a", a=1)).then_inc(adapter_in, 16)
                sp.dma_start(upT[half, :], t["up_W"]).then_inc(adapter_in, 16)

            def load_chunk(m, slot_n):
                c = index(sp, IDX_CHUNK + m, CHUNKS - 1)
                sp.dma_start(stage[:, slot_n, :], t["w"][bass.ds(c * P, P), :]).then_inc(w_in[slot_n], 16)

            def load_later(j, slot_n):
                if isinstance(j, int) and j < SLOTS_W:
                    sp.wait_ge(w_first, max(m for m in range(FIRST_CHUNKS) if m % STAGES == slot_n) + 1)
                else:
                    sp.wait_ge(w_lo, j - (SLOTS_W - 1))
                load_chunk(j + FIRST_CHUNKS, slot_n)

            def load_tile(i, parity, finished=None):
                b = [index(sp, 2 * i + (IDX_SRC + n), B - 1) for n in range(2)]
                need(sp, x_split, i - 1)
                for n in range(2):
                    sp.dma_start(x_T[:, parity, :, S * n:S * n + S],
                                 t["xT"][bass.ds(b[n] * P, P), :].rearrange("p (k s) -> p k s", k=KD))\
                      .then_inc(xT_in[parity], 16)
                if finished:
                    finished()
                need(sp, xbo_done, i - 1)
                for n in range(2):
                    sp.dma_start(x_nat[S * n:S * n + S, parity, :], t["x"][bass.ds(b[n] * S, S), :])\
                      .then_inc(xnat_in[parity], 16)

            sp.wait_ge(idx_ready, CHUNK_READY)
            for m in range(NCH // 2):
                load_chunk(m, m)
            sp.wait_ge(idx_ready, SRC_READY)
            load_tile(0, 0)
            for m in range(NCH // 2, STAGES):
                load_chunk(m, m)
            for m in range(STAGES, FIRST_CHUNKS):
                sp.wait_ge(w_first, m - STAGES + 1)
                load_chunk(m, m % STAGES)
            load_tile(1, 1)
            for j in range(AHEAD):
                load_later(j, j)
            for dst, name in ((g_t, "gamma"), (be_t, "beta"), (upb, "up_b"), (lng, "ln_gamma"), (lnb, "ln_beta")):
                sp.dma_start(dst[:, :], t[name].partition_broadcast(P)).then_inc(tables_in, 16)
            sp.wait_ge(idx_ready, ALL_READY)

            def step(i, parity, weights):
                if weights:
                    load_later(i + AHEAD, weights[2])
                def store():
                    sp.wait_ge(y_done, i - 3)
                    for n in range(2):
                        b = index(sp, 2 * i + (IDX_DST + n - 8), SLOTS - 1)
                        sp.dma_start(t["out"][bass.ds(b * S, S), :], y[S * n:S * n + S, parity, :])\
                          .then_inc(y_out[parity], 16)

                finished = store if tile_ok(0, i - 4) else None
                if tile_ok(0, i + 2):
                    load_tile(i + 2, parity, finished)
                elif finished:
                    finished()

            run(sp, step, SLOTS_W, AHEAD)
            for n in range(2):
                sp.wait_ge(y_out[n], 16 * TILES)

        @block.gpsimd
        def _(pool):
            pool.iota(iota_p[:, 0:1], [[0, 1]], base=0, channel_multiplier=1, allow_small_or_imprecise_dtypes=True).then_inc(iota_ready, 1)
            pool.iota(iota_r[:, :], [[1, SLOTS]], base=0, channel_multiplier=0, allow_small_or_imprecise_dtypes=True).then_inc(iota_ready, 1)
            pool.iota(iota_e[:, :], [[1, E0]], base=0, channel_multiplier=0, allow_small_or_imprecise_dtypes=True).then_inc(iota_ready, 1)
            pool.memset(iota_p[:, 1:2], 1.0).then_inc(iota_ready, 1)
            pool.memset(ones[:, :], 1.0).then_inc(iota_ready, 1)
            pool.iota(below[:, :], [[1, P]], base=0, channel_multiplier=-1, allow_small_or_imprecise_dtypes=True).then_inc(iota_ready, 1)
            pool.iota(lower_e[:, :, :], [[1, E0], [-1, E0]], base=0, channel_multiplier=0, allow_small_or_imprecise_dtypes=True).then_inc(iota_ready, 1)
            pool.memset(neg_half[:, 0:1], -0.5).then_inc(const_ready, 1)
            pool.memset(eps[:, 0:1], EPS0).then_inc(const_ready, 1)
            pool.memset(eps[:, 1:2], EPS1).then_inc(const_ready, 1)
            pool.memset(ada_tile[:, :, :], 0.0).then_inc(const_ready, 1)
            pool.memset(a2[:, :], 0.0).then_inc(const_ready, 1)
            n_pool = [0]

            def link(ins):
                n_pool[0] += 1
                ins.then_inc(pool_step, 1)
                pool.wait_ge(pool_step, n_pool[0])

            pool.wait_ge(iota_ready, 7)
            pool.wait_ge(const_ready, 5)
            link(pool.memset(ada[:, E1:ENTRIES, :], 0.0))
            for n in range(2):
                for e in range(E1, ENTRIES):
                    eye = ada[HALF[n], e, MAT[n]]
                    link(pool.affine_select(out=eye, in_=eye, compare_op=ALU.not_equal, fill=1.0, base=0,
                                            pattern=[[-1, A]], channel_multiplier=1))
            pool.wait_ge(ada_in, 6 * 16)
            for n in range(2):
                col = ada[HALF[n], :, COL[n]].rearrange("p e a -> p (e a)")
                link(pool.tensor_copy(col[:, E1:E1 + 1], emb[HALF[n], 0:1]))
                link(pool.tensor_copy(col[:, E1 + 1:E1 + 2], emb[HALF[n], E1 - 1:E1]))
                link(pool.tensor_tensor(col[:, 0:E1], exb[HALF[n], :], emb[HALF[n], :], ALU.add))
            pool.sem_inc(ada_ready, 1)
            pool.wait_ge(idx_ready, ALL_READY)
            pool.wait_ge(cols_in, 2 * 16)
            pool.wait_ge(bo_in, 16)

            def gather_bi(i, parity):
                e = index(pool, i + IDX_EXP, E0 - 1)
                need(pool, gelu_half, 2 * i - 2)
                pool.tensor_copy(bi_tile[:, parity, :], bi_c[:, bass.ds(e * KI, KI)]).then_inc(bi_done, 1)

            gather_bi(0, 0)
            def shift_tables():
                pool.wait_ge(tables_in, 5 * 16)
                for e in range(E0):
                    pool.tensor_tensor(be_t[:, e * D:e * D + D], be_t[:, e * D:e * D + D], upb[:, :], ALU.add)\
                        .then_inc(tables_ready, 1)
                pool.wait_ge(tables_ready, E0)

            def step(i, parity, weights):
                if isinstance(i, int) and i == 1:
                    shift_tables()
                if tile_ok(0, i - 4):
                    pool.wait_ge(z2_done, i - 3)
                    if not isinstance(i, int) or i >= 6:
                        pool.wait_ge(y_out[parity], loads(i - 6, parity, 2))
                    pool.tensor_tensor(y[:, parity, :], z2[:, :], lng[:, :], ALU.mult).then_inc(zg_done, 1)
                    pool.wait_ge(zg_done, i - 3)
                    pool.tensor_tensor(y[:, parity, :], y[:, parity, :], lnb[:, :], ALU.add).then_inc(y_done, 1)
                if tile_ok(0, i - 2):
                    pool.wait_ge(mv1_done, i - 1)
                    pool.tensor_tensor(ve1[:, :], mv1[:, 1:2], eps[:, 0:1], ALU.add).then_inc(ve1_done, 1)
                    pool.wait_ge(ve1_done, i - 1)
                    pool.tensor_tensor(rs1[:, :], ve1[:, :], neg_half[:, 0:1], ALU.pow).then_inc(rs1_done, 1)
                if tile_ok(0, i):
                    e = index(pool, i + IDX_EXP, E0 - 1)
                    pool.wait_ge(xnat_in[parity], loads(i, parity, 2))
                    pool.tensor_tensor(x_bo[:, parity, :], x_nat[:, parity, :], bo_t[:, bass.ds(e * D, D)],
                                       ALU.add).then_inc(xbo_done, 1)
                if tile_ok(0, i - 2):
                    e = index(pool, i + (IDX_EXP - 2), E0 - 1)
                    need(pool, yT_done, i - 2)
                    pool.tensor_copy(gb_tile[:, :], gb_c[:, bass.ds(e * 2 * KD, 2 * KD)]).then_inc(gb_done, 1)
                    pool.wait_ge(z1_done, i - 1)
                    pool.tensor_tensor(y_up[:, parity, :], z1[:, :], g_t[:, bass.ds(e * D, D)], ALU.mult)\
                        .then_inc(yg_done, 1)
                    pool.wait_ge(yg_done, i - 1)
                    pool.tensor_tensor(y_up[:, parity, :], y_up[:, parity, :], be_t[:, bass.ds(e * D, D)], ALU.add)\
                        .then_inc(yup_done, 1)
                if tile_ok(0, i + 1):
                    gather_bi(i + 1, 1 - parity)
                if tile_ok(0, i - 3):
                    pool.wait_ge(mv2_done, i - 2)
                    pool.tensor_tensor(ve2[:, :], mv2[:, 1:2], eps[:, 1:2], ALU.add).then_inc(ve2_done, 1)
                    pool.wait_ge(ve2_done, i - 2)
                    pool.tensor_tensor(rs2[:, :], ve2[:, :], neg_half[:, 0:1], ALU.pow).then_inc(rs2_done, 1)

            run(pool, step)

        @block.scalar
        def _(act):
            def chunk_high(c, place_n, slot_n):
                return nc.scalar.activation(W[c][:, bass.ds(place_n, 1), :, 0, :],
                                            stage[:, slot_n, :].rearrange("p (a u q) -> p a u q", a=1, u=2),
                                            ACT.Copy, scale=WS)

            act.wait_ge(const_ready, 5)
            nc.scalar.activation(neg_half[:, 1:2], neg_half[:, 0:1], ACT.Gelu)
            for m in range(FIRST_CHUNKS):
                act.wait_ge(w_in[m % STAGES], 16 * (m // STAGES + 1))
                chunk_high(m % NCH, m // NCH, m % STAGES).then_inc(w_first_hi, 1)

            def gelu(i, parity, half):
                if half == 0:
                    act.wait_ge(bi_done, i + 1)
                act.wait_ge(s1_half, 2 * i + (half + 1))
                need(act, hlo_half, 2 * i + (half - 1))
                for c in range(half * KI // 2, (half + 1) * KI // 2):
                    ins = nc.scalar.activation(h[:, c, :], p_h[parity][:, c, :], ACT.Gelu,
                                               bias=bi_tile[:, parity, c:c + 1], scale=1.0 / (XS * WS))
                ins.then_inc(gelu_half, 1)

            def high_h(i, parity, half):
                cols = slice(half * KI // 2, (half + 1) * KI // 2)
                act.wait_ge(gelu_half, 2 * i + (half + 1))
                nc.scalar.activation(h_hi[:, parity, cols, :], h[:, cols, :], ACT.Copy, scale=HS).then_inc(hhi_half, 1)

            def step(i, parity, weights):
                if tile_ok(0, i - 3):
                    need(act, a2_done, 2 * i - 6)
                    for n in range(2):
                        d = index(act, 2 * i + (IDX_DOM + n - 6), ENTRIES - 1)
                        nc.scalar.copy(ada_tile[HALF[n], n, :], ada[HALF[n], bass.ds(d, 1), :]).then_inc(ada_done, 1)
                    act.wait_ge(down_done, i - 2)
                    for n in range(2):
                        half = HALF[n]
                        nc.scalar.activation(a1[half, :], p_d[half, S * n:S * n + S], ACT.Gelu,
                                             bias=downb[half, :]).then_inc(a1_done, 1)
                if tile_ok(0, i):
                    gelu(i, parity, 0)
                    high_h(i, parity, 0)
                if weights:
                    act.wait_ge(w_in[weights[2]], w_loads(i, weights[2]))
                    chunk_high(*weights).then_inc(w_hi, 1)
                if tile_ok(0, i):
                    gelu(i, parity, 1)
                if tile_ok(0, i - 2):
                    act.wait_ge(tr_done, i - 1)
                    act.wait_ge(gb_done, i - 1)
                    for k in range(KD):
                        ins = nc.scalar.activation(yT[:, k, :], p_t[:, k * P:k * P + P], ACT.Identity,
                                                   bias=gb_tile[:, KD + k:KD + k + 1], scale=gb_tile[:, k:k + 1])
                    ins.then_inc(yT_done, 1)
                if tile_ok(0, i):
                    high_h(i, parity, 1)

            act.wait_ge(idx_ready, ALL_READY)
            act.wait_ge(ada_ready, 1)
            act.wait_ge(adapter_in, 8 * 16)
            run(act, step, NCH)

        @block.vector
        def _(dve):
            n_sort = [0]

            def link(ins):
                n_sort[0] += 1
                ins.then_inc(sort_step, 1)
                dve.wait_ge(sort_step, n_sort[0])

            v = nc.vector

            def wide(a):
                return a.unsqueeze(2).to_broadcast([a.shape[0], a.shape[1], E0])

            def rows(a, n):
                return a.unsqueeze(1).to_broadcast([a.shape[0], n, a.shape[1]])

            dve.wait_ge(tok_in, 32)
            dve.wait_ge(iota_ready, 7)
            link(v.tensor_copy(tok[:, :], tok_i[:, :]))
            link(v.tensor_scalar(tmp[:, 0:1], tok[:, 0:1], 0.0, float(E0), ALU.is_lt, ALU.mult))
            link(v.tensor_tensor(tmp[:, 1:2], tok[:, 0:1], tmp[:, 0:1], ALU.add))
            link(v.tensor_scalar(tok[:, 0:1], tmp[:, 1:2], 0.0, float(E0 - 1), ALU.max, ALU.min))
            link(v.tensor_scalar(tmp[:, 2:3], tok[:, 1:2], -1.0, float(E1), ALU.max, ALU.min))
            link(v.tensor_scalar(tmp[:, 0:1], tmp[:, 2:3], 0.0, float(E1 + 1), ALU.is_lt, ALU.mult))
            link(v.tensor_scalar(tmp[:, 1:2], tmp[:, 2:3], float(E1), None, ALU.is_ge))
            link(v.tensor_tensor(tmp[:, 3:4], tmp[:, 2:3], tmp[:, 0:1], ALU.add))
            link(v.tensor_tensor(iota_p[:, 2:3], tmp[:, 3:4], tmp[:, 1:2], ALU.add))
            link(v.tensor_scalar(ident[:, :], below[:, :], 0.0, None, ALU.is_equal))
            link(v.tensor_scalar(below[:, :], below[:, :], 0.0, None, ALU.is_gt))
            link(v.tensor_scalar(lower_e[:, :, :], lower_e[:, :, :], 0.0, None, ALU.is_gt))
            v.tensor_scalar(onehot[:, :], iota_e[:, :], tok[:, 0:1], None, ALU.is_equal).then_inc(counts_ready, 1)
            dve.wait_ge(counts_ready, 2)
            link(v.tensor_scalar(pairs_i[:, :], p_o[:, E0:2 * E0], 1.0, None, ALU.add))
            link(v.tensor_scalar(pairs_h[:, :], pairs_i[:, :], 1, None, ALU.logical_shift_right))
            link(v.tensor_copy(pairs[:, :], pairs_h[:, :]))
            link(v.tensor_tensor(ahead[:, :, :], rows(pairs[:, :], E0), wide(pairs[:, :]), ALU.is_gt))
            link(v.tensor_tensor(same[:, :, :], rows(pairs[:, :], E0), wide(pairs[:, :]), ALU.is_equal))
            link(v.tensor_tensor(same[:, :, :], same[:, :, :], lower_e[:, :, :], ALU.mult))
            link(v.tensor_tensor(ahead[:, :, :], ahead[:, :, :], same[:, :, :], ALU.add))
            link(v.tensor_reduce(place[:, :], ahead[:, :, :], AX.X, ALU.add))
            link(v.tensor_tensor(same[:, :, :], ahead[:, :, :], rows(pairs[:, :], E0), ALU.mult))
            link(v.tensor_reduce(first[:, :], same[:, :, :], AX.X, ALU.add))
            link(v.tensor_tensor(last[:, :], first[:, :], pairs[:, :], ALU.add))
            link(v.scalar_tensor_tensor(where[:, :], first[:, :], 2.0, p_o[:, 0:E0], ALU.mult, ALU.add))
            link(v.tensor_tensor(where[:, :], where[:, :], onehot[:, :], ALU.mult))
            link(v.tensor_reduce(slot[:, :], where[:, :], AX.X, ALU.add))
            link(v.tensor_scalar(at_slot[:, :], iota_r[:, :], slot[:, :], None, ALU.is_equal))
            v.tensor_scalar(before[:, :], iota_r[:, :], slot[:, :], None, ALU.is_gt).then_inc(slots_ready, 1)
            link(v.tensor_tensor(cube[:, 0:E0, :], rows(place[0:1, :], E0), wide(iota_r[0:1, 0:E0]), ALU.is_equal))
            link(v.tensor_tensor(cube[:, 0:E0, :], cube[:, 0:E0, :], rows(iota_e[0:1, :], E0), ALU.mult))
            link(v.tensor_reduce(ord_f[:, :], cube[:, 0:E0, :], AX.X, ALU.add))
            link(v.scalar_tensor_tensor(chunk_f[:, :, :], wide(ord_f[:, :]), float(NCH), rows(iota_e[0:1, :], E0),
                                        ALU.mult, ALU.add))
            v.tensor_copy(idx[:, IDX_CHUNK:IDX_LEN], chunk_f[:, :, :].rearrange("a e c -> a (e c)")).then_inc(idx_ready, 1)
            dve.wait_ge(rows_ready, 1)
            v.tensor_copy(idx[:, IDX_SRC:IDX_DST], p_t[0:1, 0:SLOTS]).then_inc(idx_ready, 1)
            link(v.tensor_tensor(cube[:, :, :], rows(last[0:1, :], TILES), wide(iota_r[0:1, 0:TILES]), ALU.is_le))
            link(v.tensor_reduce(pos_f[:, :], cube[:, :, :], AX.X, ALU.add))
            link(v.tensor_scalar(pos_f[:, :], pos_f[:, :], float(E0 - 1), None, ALU.min))
            link(v.tensor_scalar(idx[:, IDX_POS:IDX_EXP], pos_f[:, :], float(PLACE), None, ALU.mult))
            link(v.tensor_tensor(cube[:, :, :], rows(place[0:1, :], TILES), wide(pos_f[:, :]), ALU.is_equal))
            link(v.tensor_tensor(cube[:, :, :], cube[:, :, :], rows(iota_e[0:1, :], TILES), ALU.mult))
            link(v.tensor_reduce(exp_f[:, :], cube[:, :, :], AX.X, ALU.add))
            v.tensor_copy(idx[:, IDX_EXP:IDX_CHUNK], exp_f[:, :]).then_inc(idx_ready, 1)
            link(v.tensor_copy(idx[:, IDX_DOM:IDX_POS], p_d[0:1, 0:SLOTS]))
            link(v.tensor_tensor(row[:, 0, :], iota_r[0:1, :], p_u[0:1, 0:SLOTS], ALU.subtract))
            link(v.tensor_scalar(row[:, 1, :], p_o[0:1, 0:SLOTS], -1.0, 1.0, ALU.mult, ALU.add))
            link(v.scalar_tensor_tensor(row[:, 2, :], row[:, 0, :], float(B), row[:, 1, :], ALU.add, ALU.mult))
            link(v.tensor_tensor(row[:, 3, :], row[:, 2, :], p_t[0:1, 0:SLOTS], ALU.add))
            v.tensor_copy(idx[:, IDX_DST:IDX_DOM], row[:, 3, :]).then_inc(idx_ready, 1)

            def high_x(i, parity):
                dve.wait_ge(xT_in[parity], loads(i, parity, 2))
                v.tensor_scalar(x_hi[:, parity, :, :], x_T[:, parity, :, :], XS, None, ALU.mult).then_inc(xhi_done, 1)

            def low_x(i, parity):
                dve.wait_ge(xhi_done, i + 1)
                v.scalar_tensor_tensor(x_lo[:, parity, :, :], x_T[:, parity, :, :], XS, x_hi[:, parity, :, :],
                                       ALU.mult, ALU.subtract).then_inc(x_split, 1)

            def chunk_low(c, place_n, slot_n):
                return v.scalar_tensor_tensor(W[c][:, bass.ds(place_n, 1), :, 1, :],
                                              stage[:, slot_n, :].rearrange("p (a u q) -> p a u q", a=1, u=2),
                                              WS, W[c][:, bass.ds(place_n, 1), :, 0, :], ALU.mult, ALU.subtract)

            for m in range(FIRST_CHUNKS):
                dve.wait_ge(w_first_hi, m + 1)
                chunk_low(m % NCH, m // NCH, m % STAGES).then_inc(w_first, 1)
                if m == 0:
                    high_x(0, 0)
                    low_x(0, 0)

            def split_h(i, parity, half):
                cols = slice(half * KI // 2, (half + 1) * KI // 2)
                dve.wait_ge(hhi_half, 2 * i + (half + 1))
                v.scalar_tensor_tensor(h_lo[:, parity, cols, :], h[:, cols, :], HS, h_hi[:, parity, cols, :],
                                       ALU.mult, ALU.subtract).then_inc(hlo_half, 1)

            def step(i, parity, weights):
                if tile_ok(0, i - 2):
                    dve.wait_ge(s2_done, i - 1)
                    dve.wait_ge(xbo_done, i - 1)
                    v.scalar_tensor_tensor(r1[:, :], p_o[:, 0:D], 1.0 / (HS * WS), x_bo[:, parity, :],
                                           ALU.mult, ALU.add).then_inc(r1_part, 1)
                    dve.wait_ge(r1_part, i - 1)
                    v.scalar_tensor_tensor(r1[:, :], p_o[:, D:2 * D], 1.0 / (HS * WS), r1[:, :],
                                           ALU.mult, ALU.add).then_inc(r1_done, 1)
                    dve.wait_ge(r1_done, i - 1)
                    v.bn_stats(st1[:, :], r1[:, :]).then_inc(st1_done, 1)
                if tile_ok(0, i - 2):
                    dve.wait_ge(st1_done, i - 1)
                if tile_ok(0, i + 1):
                    high_x(i + 1, 1 - parity)
                if tile_ok(0, i - 2):
                    v.bn_aggr(mv1[:, :], st1[:, :]).then_inc(mv1_done, 1)
                if tile_ok(0, i - 3):
                    dve.wait_ge(exp_done, i - 2)
                    for n in range(2):
                        half = HALF[n]
                        v.tensor_scalar(a2[half, S * n:S * n + S], p_d[half, P:P + S], ada_tile[half, n, COL[n]],
                                        None, ALU.add).then_inc(a2_done, 1)
                if tile_ok(0, i - 2):
                    dve.wait_ge(rs1_done, i - 1)
                    v.tensor_scalar(z1[:, :], r1[:, :], mv1[:, 0:1], rs1[:, :], ALU.subtract, ALU.mult)\
                        .then_inc(z1_done, 1)
                if tile_ok(0, i):
                    split_h(i, parity, 0)
                if tile_ok(0, i - 3):
                    dve.wait_ge(up_done, i - 2)
                    dve.wait_ge(yup_done, i - 2)
                    v.tensor_tensor(r2[:, :], p_u[:, 0:D], y_up[:, 1 - parity, :], ALU.add).then_inc(r2_done, 1)
                    dve.wait_ge(r2_done, i - 2)
                    v.bn_stats(st2[:, :], r2[:, :]).then_inc(st2_done, 1)
                if tile_ok(0, i - 3):
                    dve.wait_ge(st2_done, i - 2)
                if tile_ok(0, i + 1):
                    low_x(i + 1, 1 - parity)
                if tile_ok(0, i - 3):
                    v.bn_aggr(mv2[:, :], st2[:, :]).then_inc(mv2_done, 1)
                if weights:
                    dve.wait_ge(w_hi, i + 1)
                    chunk_low(*weights).then_inc(w_lo, 1)
                if tile_ok(0, i):
                    split_h(i, parity, 1)
                if tile_ok(0, i - 3):
                    dve.wait_ge(rs2_done, i - 2)
                    v.tensor_scalar(z2[:, :], r2[:, :], mv2[:, 0:1], rs2[:, :], ALU.subtract, ALU.mult)\
                        .then_inc(z2_done, 1)

            run(dve, step, NCH)

        @block.tensor
        def _(pe):
            mm = nc.tensor.matmul
            BATCH = 2
            DOWN_AT, EXP_AT, UP_AT, TR_AT = 1, 4, 9, 3
            pe.wait_ge(counts_ready, 1)
            pe.wait_ge(iota_ready, 7)
            mm(p_o[:, 0:E0], below[:, :], onehot[:, :], start=True, stop=True)
            mm(p_o[:, E0:2 * E0], ones[:, :], onehot[:, :], start=True, stop=True).then_inc(counts_ready, 1)
            pe.wait_ge(slots_ready, 1)
            mm(p_t[0:1, 0:SLOTS], iota_p[:, 0:1], at_slot[:, :], start=True, stop=True)
            mm(p_o[0:1, 0:SLOTS], iota_p[:, 1:2], at_slot[:, :], start=True, stop=True)
            mm(p_d[0:1, 0:SLOTS], iota_p[:, 2:3], at_slot[:, :], start=True, stop=True)
            mm(p_u[0:1, 0:SLOTS], iota_p[:, 1:2], before[:, :], start=True, stop=True).then_inc(rows_ready, 1)
            pe.wait_ge(idx_ready, TILE_READY)
            pe.wait_ge(const_ready, 5)

            def first_weights(place_reg, c, k):
                chunk, at = w_flat[k * 2 + c // 4], c % 4 // 2 * WCH + c % 2 * P
                return chunk[:, bass.ds(place_reg + at, P)], chunk[:, bass.ds(place_reg + (at + QC), P)]

            def second_weights(place_reg, j):
                chunk, at = w_flat[NCH // 2 + j // 2], j % 2 * WCH
                return chunk[:, bass.ds(place_reg + at, 2 * D)], chunk[:, bass.ds(place_reg + at, D)]

            def first_addresses(place_reg, cs):
                for k in range(KD):
                    for c in cs:
                        for part in first_weights(place_reg, c, k):
                            pe.lower_ap(part, for_matmul_weights=True)

            def second_addresses(place_reg, js):
                for j in js:
                    pe.lower_ap(second_weights(place_reg, j)[0])

            def first_product(parity, place_reg, c):
                for k in range(KD):
                    hi, lo = first_weights(place_reg, c, k)
                    mm(p_h[parity][:, c, :], hi, x_hi[:, parity, k, :], start=(k == 0), stop=False)
                    mm(p_h[parity][:, c, :], hi, x_lo[:, parity, k, :], start=False, stop=False)
                    ins = mm(p_h[parity][:, c, :], lo, x_hi[:, parity, k, :], start=False, stop=(k == KD - 1))
                return ins

            def second_product(parity, place_reg, j):
                both, hi = second_weights(place_reg, j)
                mm(p_o[:, :], h_hi[:, parity, j, :], both, start=(j == 0), stop=(j == KI - 1))
                return mm(p_o[:, 0:D], h_lo[:, parity, j, :], hi, start=False, stop=False, skip_group_check=True)

            def step(i, parity, weights):
                def down():
                    pe.wait_ge(yT_done, i - 2)
                    for k in range(KD):
                        ins = mm(p_d[:, 0:P], downT[:, k, :, :], yT[:, k, :], start=(k == 0), stop=(k == KD - 1))
                    ins.then_inc(down_done, 1)

                def expert():
                    pe.wait_ge(a1_done, 2 * i - 4)
                    mm(p_d[:, P:P + S], ada_tile[:, :, :].rearrange("p n a -> p (n a)")[:, 1:2 * A + 1], a1[:, :],
                       start=True, stop=True).then_inc(exp_done, 1)

                def up():
                    pe.wait_ge(a2_done, 2 * i - 4)
                    mm(p_u[:, 0:D], a2[:, :], upT[:, :], start=True, stop=True).then_inc(up_done, 1)

                def transpose():
                    pe.wait_ge(z1_done, i - 1)
                    for k in range(KD):
                        ins = nc.tensor.transpose(p_t[:, k * P:k * P + P], z1[:, k * P:k * P + P], ident[:, :])
                    ins.then_inc(tr_done, 1)

                between = {DOWN_AT: down, EXP_AT: expert, UP_AT: up} if tile_ok(0, i - 3) else {}
                if tile_ok(0, i):
                    here = index(pe, i + IDX_POS, (E0 - 1) * PLACE)
                    first_addresses(here, range(2))
                    pe.wait_ge(x_split, i + 1)
                    if isinstance(i, int) and i == 0:
                        pe.wait_ge(w_first, NCH // 2)
                for c in range(KI):
                    if tile_ok(0, i):
                        if c in (1, 3, 5):
                            first_addresses(here, range(c + 1, c + 3))
                        ins = first_product(parity, here, c)
                        if c % (KI // 2) == KI // 2 - 1:
                            ins.then_inc(s1_half, 1)
                    if tile_ok(0, i - 1):
                        if c == 0:
                            there = index(pe, i + (IDX_POS - 1), (E0 - 1) * PLACE)
                        if c in (2, 4):
                            second_addresses(there, range(2 * c - 4, 2 * c))
                    if c in between:
                        between[c]()
                if tile_ok(0, i - 1):
                    if isinstance(i, int) and i == 1:
                        pe.wait_ge(w_first, FIRST_CHUNKS)
                    elif weights:
                        pe.wait_ge(w_lo, i - 1)
                    else:
                        pe.wait_ge(w_lo, CHUNKS - FIRST_CHUNKS)
                    pe.wait_ge(hlo_half, 2 * i)
                    need(pe, r1_done, i - 1)
                for j in range(KI):
                    if j + KI in between:
                        between[j + KI]()
                    if j == TR_AT and tile_ok(0, i - 2):
                        transpose()
                    if tile_ok(0, i - 1):
                        ins = second_product(1 - parity, there, j)
                        if j == KI - 1:
                            ins.then_inc(s2_done, 1)

            pe.wait_ge(adapter_in, 8 * 16)
            run(pe, step)


def kernel(x, itok_B_0_7, itok_B_0_15, L0_cond_Wi, L0_cond_bi, L0_cond_Wo, L0_cond_bo, L0_cond_gamma,
           L0_cond_beta, L1_cond_down_W, L1_cond_down_b, L1_cond_up_W, L1_cond_up_b, L1_cond_expert_W,
           L1_cond_expert_b, L1_cond_domain_emb, L1_cond_ln_gamma, L1_cond_ln_beta):
    import numpy as np
    import concourse.bacc as bacc
    from concourse.bass_utils import run_bass_kernel_spmd

    wi = np.asarray(L0_cond_Wi).reshape(E0, KD, P, I // WCH, WCH).transpose(0, 1, 3, 2, 4)
    wo = np.asarray(L0_cond_Wo).reshape(E0, NCH // 2, WCH // D, P, D).transpose(0, 1, 3, 2, 4)
    w = np.concatenate([wi.reshape(E0, NCH // 2, P, WCH), wo.reshape(E0, NCH // 2, P, WCH)], axis=1)
    g = np.asarray(L0_cond_gamma).reshape(E0, KD, P).transpose(2, 0, 1)
    be = np.asarray(L0_cond_beta).reshape(E0, KD, P).transpose(2, 0, 1)
    arrays = {
        "itok0": itok_B_0_7,
        "itok1": itok_B_0_15,
        "x": np.asarray(x).reshape(B * S, D),
        "xT": np.asarray(x).reshape(B, S, KD, P).transpose(0, 3, 2, 1).reshape(B * P, KD * S),
        "w": w.reshape(CHUNKS * P, WCH),
        "bi": np.asarray(L0_cond_bi).reshape(E0, KI, P).transpose(2, 0, 1).reshape(P, E0 * KI),
        "gb": np.concatenate([g, be], axis=2).reshape(P, E0 * 2 * KD),
        "bo": np.asarray(L0_cond_bo).reshape(E0 * D),
        "gamma": np.asarray(L0_cond_gamma).reshape(E0 * D),
        "beta": np.asarray(L0_cond_beta).reshape(E0 * D),
        "down_W": np.asarray(L1_cond_down_W).T,
        "down_b": L1_cond_down_b,
        "up_W": np.asarray(L1_cond_up_W).T,
        "up_b": L1_cond_up_b,
        "expert_W": np.asarray(L1_cond_expert_W).transpose(2, 0, 1),
        "expert_b": np.asarray(L1_cond_expert_b).T,
        "emb": np.asarray(L1_cond_domain_emb).T,
        "ln_gamma": L1_cond_ln_gamma,
        "ln_beta": L1_cond_ln_beta,
    }
    nc = bacc.Bacc("TRN2", target_bir_lowering=False, num_devices=1)
    fed, t = {}, {}
    for name, a in arrays.items():
        a = np.ascontiguousarray(a)
        fed[f"in_{name}"] = a
        t[name] = nc.dram_tensor(f"in_{name}", a.shape, mybir.dt.from_np(a.dtype), kind="ExternalInput").ap()
    t["out"] = nc.dram_tensor("out", (SLOTS * S, D), mybir.dt.float32, kind="ExternalOutput").ap()
    build(nc, t)
    got = run_bass_kernel_spmd(nc, [fed], core_ids=[0]).results[0]["out"]
    return got.reshape(SLOTS, S, D)[:B]
```

```python
import concourse.bass as bass
from concourse import mybir
from contextlib import ExitStack

B, S, D = 128, 64, 256
E0, I = 8, 1024
E1, A = 16, 64
P = 128
KD, KI = D // P, I // P
TILES = B // 2 + E0 // 2
SLOTS = 2 * TILES
ENTRIES = E1 + 2
WCH, NCH = 512, 8
CHUNKS = E0 * NCH
QC = WCH // 2
FIRST_CHUNKS = NCH
STAGES = 6
SLOTS_W = 4
XS, HS, WS = 8.0, 8.0, 512.0
EPS0, EPS1 = 1e-12, 1e-5
LEAD = NCH
STEPS = TILES + 4

IDX_SRC, IDX_DST, IDX_DOM = 0, SLOTS, 2 * SLOTS
IDX_POS = 3 * SLOTS
IDX_EXP = IDX_POS + TILES
IDX_CHUNK = IDX_EXP + TILES
IDX_LEN = IDX_CHUNK + CHUNKS


def build(nc, t):
    fp32, f16, i32 = mybir.dt.float32, mybir.dt.float16, mybir.dt.int32
    ALU, ACT, AX = mybir.AluOpType, mybir.ActivationFunctionType, mybir.AxisListType

    ctx = ExitStack()
    with ctx:
        def sb(name, shape, dt=fp32):
            return ctx.enter_context(nc.sbuf_tensor(name, shape, dt))

        def pb(name, shape):
            return ctx.enter_context(nc.psum_tensor(name, shape, fp32))

        def sem(name):
            return ctx.enter_context(nc.semaphore(name))

        W = [sb(f"W{c}", [P, E0, 2, 2, QC], f16) for c in range(NCH)]
        w_flat = [w[:, :, :, :, :].rearrange("p e u r q -> p (e u r q)") for w in W]
        PLACE = 2 * WCH
        stage = sb("stage", [P, STAGES, WCH])
        bo_t = sb("bo_t", [P, E0 * D])
        g_t = sb("g_t", [P, E0 * D])
        be_t = sb("be_t", [P, E0 * D])
        bi_c = sb("bi_c", [P, E0 * KI])
        gb_c = sb("gb_c", [P, E0 * 2 * KD])
        lng = sb("lng", [P, D])
        lnb = sb("lnb", [P, D])
        upb = sb("upb", [P, D])
        upT = sb("upT", [P, D])
        downT = sb("downT", [P, KD, 2, A])
        downb = sb("downb", [P, 1])
        ada = sb("ada", [P, ENTRIES, A + 1])
        emb = sb("emb", [P, E1])
        ident = sb("ident", [P, P])

        x_nat = sb("x_nat", [P, 2, D])
        x_T = sb("x_T", [P, 2, KD, P])
        x_hi = sb("x_hi", [P, 2, KD, P], f16)
        x_lo = sb("x_lo", [P, 2, KD, P], f16)
        x_bo = sb("x_bo", [P, 2, D])
        bi_tile = sb("bi_tile", [P, 2, KI])
        h = sb("h", [P, KI, P])
        h_hi = sb("h_hi", [P, 2, KI, P], f16)
        h_lo = sb("h_lo", [P, 2, KI, P], f16)
        r1 = sb("r1", [P, D])
        st1 = sb("st1", [P, 6])
        mv1 = sb("mv1", [P, 2])
        ve1 = sb("ve1", [P, 1])
        rs1 = sb("rs1", [P, 1])
        z1 = sb("z1", [P, D])
        gb_tile = sb("gb_tile", [P, 2 * KD])
        yT = sb("yT", [P, KD, P])
        y_up = sb("y_up", [P, 2, D])
        a1 = sb("a1", [P, S])
        ada_tile = sb("ada_tile", [P, 2, A + 1])
        a2 = sb("a2", [P, P])
        r2 = sb("r2", [P, D])
        st2 = sb("st2", [P, 6])
        mv2 = sb("mv2", [P, 2])
        ve2 = sb("ve2", [P, 1])
        rs2 = sb("rs2", [P, 1])
        z2 = sb("z2", [P, D])
        y = sb("y", [P, 2, D])
        neg_half = sb("neg_half", [P, 2])
        eps = sb("eps", [P, 2])

        taken = {"h": 0, "x_bo": 0}
        homes = {"h": h[:, :, :].rearrange("p c q -> p (c q)"), "x_bo": x_bo[:, :, :].rearrange("p c q -> p (c q)")}

        def early(*shape, home="h"):
            n = shape[0] if len(shape) == 1 else shape[0] * shape[1]
            a = homes[home][:, taken[home]:taken[home] + n]
            taken[home] += n
            return a if len(shape) == 1 else a.rearrange("p (a b) -> p a b", b=shape[1])

        iota_r = early(SLOTS)
        at_slot = early(SLOTS)
        before = early(SLOTS)
        below = early(P)
        ones = early(P)
        lower_e = early(E0, E0)
        ahead = early(E0, E0)
        same = early(E0, E0)
        cube = h_hi[0:1, :, :, :].rearrange("p a c q -> p (a c q)").bitcast(fp32)[:, 0:TILES * E0]\
            .rearrange("p (t e) -> p t e", e=E0)
        row = h_lo[0:1, :, :, :].rearrange("p a c q -> p (a c q)").bitcast(fp32)[:, 0:4 * SLOTS]\
            .rearrange("p (t e) -> p t e", e=SLOTS)
        tok_i = sb("tok_i", [P, 2], i32)
        tok = sb("tok", [P, 2])
        tmp = sb("tmp", [P, 4])
        iota_p = sb("iota_p", [P, 3])
        iota_e = early(E0, home="x_bo")
        exb = early(E1, home="x_bo")
        onehot = early(E0, home="x_bo")
        pairs_i = sb("pairs_i", [P, E0], i32)
        pairs_h = sb("pairs_h", [P, E0], i32)
        pairs = early(E0, home="x_bo")
        place = early(E0, home="x_bo")
        first = early(E0, home="x_bo")
        last = early(E0, home="x_bo")
        where = early(E0, home="x_bo")
        slot = sb("slot", [P, 1])
        pos_f = early(TILES)[0:1]
        exp_f = early(TILES)[0:1]
        ord_f = early(E0, home="x_bo")[0:1]
        chunk_f = early(E0, NCH, home="x_bo")[0:1]
        idx = sb("idx", [1, IDX_LEN], i32)

        p_h = [pb(f"p_h{n}", [P, KI, P]) for n in range(2)]
        p_o = pb("p_o", [P, 512])
        p_t = pb("p_t", [P, 512])
        p_d = pb("p_d", [P, 512])
        p_u = pb("p_u", [P, 512])

        tok_in = sem("tok_in")
        cols_in = sem("cols_in")
        bo_in = sem("bo_in")
        adapter_in = sem("adapter_in")
        tables_in = sem("tables_in")
        ada_in = sem("ada_in")
        w_in = [sem(f"w_in{n}") for n in range(STAGES)]
        xnat_in = [sem(f"xnat_in{n}") for n in range(2)]
        xT_in = [sem(f"xT_in{n}") for n in range(2)]
        y_out = [sem(f"y_out{n}") for n in range(2)]
        CHUNK_READY, SRC_READY, TILE_READY, ALL_READY = 1, 2, 3, 4
        iota_ready = sem("iota_ready")
        const_ready = sem("const_ready")
        sort_step = sem("sort_step")
        pool_step = sem("pool_step")
        counts_ready = sem("counts_ready")
        slots_ready = sem("slots_ready")
        rows_ready = sem("rows_ready")
        idx_ready = sem("idx_ready")
        ada_ready = sem("ada_ready")
        tables_ready = sem("tables_ready")
        w_first_hi = sem("w_first_hi")
        w_first = sem("w_first")
        w_hi = sem("w_hi")
        w_lo = sem("w_lo")
        xhi_done = sem("xhi_done")
        x_split = sem("x_split")
        xbo_done = sem("xbo_done")
        bi_done = sem("bi_done")
        s1_half = sem("s1_half")
        gelu_half = sem("gelu_half")
        hhi_half = sem("hhi_half")
        hlo_half = sem("hlo_half")
        s2_done = sem("s2_done")
        r1_done = sem("r1_done")
        st1_done = sem("st1_done")
        mv1_done = sem("mv1_done")
        ve1_done = sem("ve1_done")
        rs1_done = sem("rs1_done")
        z1_done = sem("z1_done")
        tr_done = sem("tr_done")
        gb_done = sem("gb_done")
        yT_done = sem("yT_done")
        yg_done = sem("yg_done")
        yup_part = sem("yup_part")
        yup_done = sem("yup_done")
        down_done = sem("down_done")
        a1_done = sem("a1_done")
        ada_done = sem("ada_done")
        exp_done = sem("exp_done")
        a2_done = sem("a2_done")
        up_done = sem("up_done")
        r2_done = sem("r2_done")
        st2_done = sem("st2_done")
        mv2_done = sem("mv2_done")
        ve2_done = sem("ve2_done")
        rs2_done = sem("rs2_done")
        z2_done = sem("z2_done")
        zg_done = sem("zg_done")
        y_done = sem("y_done")

        block = ctx.enter_context(nc.Block())

        def need(eng, s, value):
            if isinstance(value, int) and value <= 0:
                return
            eng.wait_ge(s, value)

        def index(eng, at, top):
            return nc.values_load(idx[0:1, bass.ds(at, 1)], engines=[eng.engine], min_val=0, max_val=top,
                                  skip_runtime_bounds_check_because="the sorting clips every index")

        def indices(eng, at, count, top):
            return nc.values_load_multi_w_load_instructions(
                idx[0:1, bass.ds(at, count)], engines=[eng.engine], min_val=0, max_val=top,
                skip_runtime_bounds_check_because="the sorting clips every index")[1]

        HALF = [slice(0, A), slice(A, 2 * A)]
        MAT = [slice(1, A + 1), slice(0, A)]
        COL = [slice(0, 1), slice(A, A + 1)]

        def exists(i):
            return not isinstance(i, int) or 0 <= i < TILES

        def stage_slot(j):
            return (j + 2) % SLOTS_W

        def run(eng, step, unroll=2, ahead=0):
            lead, mid = LEAD - ahead, CHUNKS - FIRST_CHUNKS - ahead
            for i in range(lead):
                j = i + ahead
                step(i, i % 2, (j % NCH, (j + FIRST_CHUNKS) // NCH, stage_slot(j)))
            for begin, end, weights, times in ((lead, mid, True, unroll), (mid, TILES - 2, False, 2)):
                with eng.Fori(0, (end - begin) // times) as n:
                    i = eng.snap(n * times + begin)
                    for q in range(times):
                        step(i + q, q % 2, (q, n + (FIRST_CHUNKS + LEAD) // NCH, stage_slot(LEAD + q))
                             if weights else False)
            for i in range(TILES - 2, STEPS):
                step(i, i % 2, False)

        def loads(i, parity, each):
            n = 16 * each
            return ((i - parity) // 2 + 1) * n if isinstance(i, int) else (i - parity) * (n // 2) + n

        def w_loads(i, slot_n):
            early = len([m for m in range(FIRST_CHUNKS) if m % STAGES == slot_n])
            begin = [j for j in range(SLOTS_W) if stage_slot(j) == slot_n][0]
            if isinstance(i, int):
                return 16 * (early + (i - begin) // SLOTS_W + 1)
            return (i - begin) * (16 // SLOTS_W) + 16 * (early + 1)

        @block.sync
        def _(sp):
            AHEAD = 2
            sp.dma_start(tok_i[:, 0:1], t["itok0"].rearrange("(p a) -> p a", a=1)).then_inc(tok_in, 16)
            sp.dma_start(tok_i[:, 1:2], t["itok1"].rearrange("(p a) -> p a", a=1)).then_inc(tok_in, 16)
            sp.dma_start(bi_c[:, :], t["bi"]).then_inc(cols_in, 16)
            sp.dma_start(gb_c[:, :], t["gb"]).then_inc(cols_in, 16)
            for n in range(2):
                half = HALF[n]
                sp.dma_start(ada[half, 0:E1, MAT[n]], t["expert_W"]).then_inc(ada_in, 16)
                sp.dma_start(exb[half, :], t["expert_b"]).then_inc(ada_in, 16)
                sp.dma_start(emb[half, :], t["emb"]).then_inc(ada_in, 16)
            sp.dma_start(bo_t[:, :], t["bo"].partition_broadcast(P)).then_inc(bo_in, 16)
            sp.dma_start(g_t[:, :], t["gamma"].partition_broadcast(P)).then_inc(tables_in, 16)
            for n in range(2):
                half = HALF[n]
                for k in range(KD):
                    sp.dma_start(downT[:, k, n, :], t["down_W"][k * P:k * P + P, :]).then_inc(adapter_in, 16)
                sp.dma_start(downb[half, :], t["down_b"].rearrange("(p a) -> p a", a=1)).then_inc(adapter_in, 16)
                sp.dma_start(upT[half, :], t["up_W"]).then_inc(adapter_in, 16)

            def load_chunk(m, slot_n):
                c = index(sp, IDX_CHUNK + m, CHUNKS - 1)
                sp.dma_start(stage[:, slot_n, :], t["w"][bass.ds(c * P, P), :]).then_inc(w_in[slot_n], 16)

            def load_later(j, slot_n):
                if isinstance(j, int) and j < SLOTS_W:
                    sp.wait_ge(w_first, max(m for m in range(FIRST_CHUNKS) if m % STAGES == slot_n) + 1)
                else:
                    sp.wait_ge(w_lo, j - (SLOTS_W - 1))
                load_chunk(j + FIRST_CHUNKS, slot_n)

            def load_turned(b, i, parity):
                need(sp, x_split, i - 1)
                for n in range(2):
                    sp.dma_start(x_T[:, parity, :, S * n:S * n + S],
                                 t["xT"][bass.ds(b[n] * P, P), :].rearrange("p (k s) -> p k s", k=KD))\
                      .then_inc(xT_in[parity], 16)

            def load_natural(b, i, parity):
                need(sp, xbo_done, i - 1)
                for n in range(2):
                    sp.dma_start(x_nat[S * n:S * n + S, parity, :], t["x"][bass.ds(b[n] * S, S), :])\
                      .then_inc(xnat_in[parity], 16)

            sp.wait_ge(idx_ready, CHUNK_READY)
            for m in range(NCH // 2):
                load_chunk(m, m)
            sp.wait_ge(idx_ready, SRC_READY)
            b = [indices(sp, 2 * i + IDX_SRC, 2, B - 1) for i in range(2)]
            load_turned(b[0], 0, 0)
            load_turned(b[1], 1, 1)
            for m in range(NCH // 2, FIRST_CHUNKS):
                if m >= STAGES:
                    sp.wait_ge(w_first, m - STAGES + 1)
                load_chunk(m, m % STAGES)
            load_natural(b[0], 0, 0)
            load_natural(b[1], 1, 1)
            for j in range(AHEAD):
                load_later(j, stage_slot(j))
            for dst, name in ((be_t, "beta"), (upb, "up_b"), (lng, "ln_gamma"), (lnb, "ln_beta")):
                sp.dma_start(dst[:, :], t[name].partition_broadcast(P)).then_inc(tables_in, 16)
            sp.wait_ge(idx_ready, ALL_READY)

            def step(i, parity, weights):
                if weights:
                    load_later(i + AHEAD, weights[2])
                def store():
                    sp.wait_ge(y_done, i - 3)
                    b = indices(sp, 2 * i + (IDX_DST - 8), 2, SLOTS - 1)
                    for n in range(2):
                        sp.dma_start(t["out"][bass.ds(b[n] * S, S), :], y[S * n:S * n + S, parity, :])\
                          .then_inc(y_out[parity], 16)

                if exists(i + 2):
                    b = indices(sp, 2 * i + (IDX_SRC + 4), 2, B - 1)
                    load_turned(b, i + 2, parity)
                if exists(i - 4):
                    store()
                if exists(i + 2):
                    load_natural(b, i + 2, parity)

            run(sp, step, SLOTS_W, AHEAD)
            for n in range(2):
                sp.wait_ge(y_out[n], 16 * TILES)

        @block.gpsimd
        def _(pool):
            pool.iota(iota_p[:, 0:1], [[0, 1]], base=0, channel_multiplier=1,
                      allow_small_or_imprecise_dtypes=True).then_inc(iota_ready, 1)
            pool.iota(iota_r[:, :], [[1, SLOTS]], base=0, channel_multiplier=0,
                      allow_small_or_imprecise_dtypes=True).then_inc(iota_ready, 1)
            pool.iota(iota_e[:, :], [[1, E0]], base=0, channel_multiplier=0,
                      allow_small_or_imprecise_dtypes=True).then_inc(iota_ready, 1)
            pool.memset(iota_p[:, 1:2], 1.0).then_inc(iota_ready, 1)
            pool.memset(ones[:, :], 1.0).then_inc(iota_ready, 1)
            pool.iota(below[:, :], [[1, P]], base=0, channel_multiplier=-1,
                      allow_small_or_imprecise_dtypes=True).then_inc(iota_ready, 1)
            pool.iota(lower_e[:, :, :], [[1, E0], [-1, E0]], base=0, channel_multiplier=0,
                      allow_small_or_imprecise_dtypes=True).then_inc(iota_ready, 1)
            pool.memset(neg_half[:, 0:1], -0.5).then_inc(const_ready, 1)
            pool.memset(eps[:, 0:1], EPS0).then_inc(const_ready, 1)
            pool.memset(eps[:, 1:2], EPS1).then_inc(const_ready, 1)
            pool.memset(ada_tile[:, :, :], 0.0).then_inc(const_ready, 1)
            pool.memset(a2[:, :], 0.0).then_inc(const_ready, 1)
            n_pool = [0]

            def link(ins):
                n_pool[0] += 1
                ins.then_inc(pool_step, 1)
                pool.wait_ge(pool_step, n_pool[0])

            pool.wait_ge(iota_ready, 7)
            pool.wait_ge(const_ready, 5)
            link(pool.memset(ada[:, E1:ENTRIES, :], 0.0))
            for n in range(2):
                for e in range(E1, ENTRIES):
                    eye = ada[HALF[n], e, MAT[n]]
                    link(pool.affine_select(out=eye, in_=eye, compare_op=ALU.not_equal, fill=1.0, base=0,
                                            pattern=[[-1, A]], channel_multiplier=1))
            pool.wait_ge(ada_in, 6 * 16)
            for n in range(2):
                col = ada[HALF[n], :, COL[n]].rearrange("p e a -> p (e a)")
                link(pool.tensor_copy(col[:, E1:E1 + 1], emb[HALF[n], 0:1]))
                link(pool.tensor_copy(col[:, E1 + 1:E1 + 2], emb[HALF[n], E1 - 1:E1]))
                link(pool.tensor_tensor(col[:, 0:E1], exb[HALF[n], :], emb[HALF[n], :], ALU.add))
            pool.sem_inc(ada_ready, 1)
            pool.wait_ge(idx_ready, ALL_READY)
            pool.wait_ge(cols_in, 2 * 16)
            pool.wait_ge(bo_in, 16)

            def gather_bi(i, parity):
                e = index(pool, i + IDX_EXP, E0 - 1)
                need(pool, gelu_half, 2 * i - 2)
                pool.tensor_copy(bi_tile[:, parity, :], bi_c[:, bass.ds(e * KI, KI)]).then_inc(bi_done, 1)

            gather_bi(0, 0)
            def shift_tables():
                pool.wait_ge(tables_in, 5 * 16)
                for e in range(E0):
                    pool.tensor_tensor(be_t[:, e * D:e * D + D], be_t[:, e * D:e * D + D], upb[:, :], ALU.add)\
                        .then_inc(tables_ready, 1)
                pool.wait_ge(tables_ready, E0)

            def step(i, parity, weights):
                if isinstance(i, int) and i == 1:
                    shift_tables()
                if exists(i - 4):
                    pool.wait_ge(z2_done, i - 3)
                    if not isinstance(i, int) or i >= 6:
                        pool.wait_ge(y_out[parity], loads(i - 6, parity, 2))
                    pool.tensor_tensor(y[:, parity, :], z2[:, :], lng[:, :], ALU.mult).then_inc(zg_done, 1)
                    pool.wait_ge(zg_done, i - 3)
                    pool.tensor_tensor(y[:, parity, :], y[:, parity, :], lnb[:, :], ALU.add).then_inc(y_done, 1)
                if exists(i - 2):
                    pool.wait_ge(mv1_done, i - 1)
                    pool.tensor_tensor(ve1[:, :], mv1[:, 1:2], eps[:, 0:1], ALU.add).then_inc(ve1_done, 1)
                    pool.wait_ge(ve1_done, i - 1)
                    pool.tensor_tensor(rs1[:, :], ve1[:, :], neg_half[:, 0:1], ALU.pow).then_inc(rs1_done, 1)
                if exists(i):
                    e = index(pool, i + IDX_EXP, E0 - 1)
                    pool.wait_ge(xnat_in[parity], loads(i, parity, 2))
                    pool.tensor_tensor(x_bo[:, parity, :], x_nat[:, parity, :], bo_t[:, bass.ds(e * D, D)],
                                       ALU.add).then_inc(xbo_done, 1)
                if exists(i - 2):
                    e = index(pool, i + (IDX_EXP - 2), E0 - 1)
                    need(pool, yT_done, i - 2)
                    pool.tensor_copy(gb_tile[:, :], gb_c[:, bass.ds(e * 2 * KD, 2 * KD)]).then_inc(gb_done, 1)
                    pool.wait_ge(z1_done, i - 1)
                    pool.tensor_tensor(y_up[:, parity, :], z1[:, :], g_t[:, bass.ds(e * D, D)], ALU.mult)\
                        .then_inc(yg_done, 1)
                    pool.wait_ge(yg_done, i - 1)
                    pool.tensor_tensor(y_up[:, parity, :], y_up[:, parity, :], be_t[:, bass.ds(e * D, D)], ALU.add)\
                        .then_inc(yup_done, 1)
                if exists(i + 1):
                    gather_bi(i + 1, 1 - parity)
                if exists(i - 3):
                    pool.wait_ge(mv2_done, i - 2)
                    pool.tensor_tensor(ve2[:, :], mv2[:, 1:2], eps[:, 1:2], ALU.add).then_inc(ve2_done, 1)
                    pool.wait_ge(ve2_done, i - 2)
                    pool.tensor_tensor(rs2[:, :], ve2[:, :], neg_half[:, 0:1], ALU.pow).then_inc(rs2_done, 1)

            run(pool, step)

        @block.scalar
        def _(act):
            def chunk_high(c, place_n, slot_n):
                return nc.scalar.activation(W[c][:, bass.ds(place_n, 1), :, 0, :],
                                            stage[:, slot_n, :].rearrange("p (a u q) -> p a u q", a=1, u=2),
                                            ACT.Copy, scale=WS)

            act.wait_ge(const_ready, 5)
            nc.scalar.activation(neg_half[:, 1:2], neg_half[:, 0:1], ACT.Gelu)
            for m in range(FIRST_CHUNKS):
                act.wait_ge(w_in[m % STAGES], 16 * (m // STAGES + 1))
                chunk_high(m % NCH, m // NCH, m % STAGES).then_inc(w_first_hi, 1)

            def gelu(i, parity, half):
                if half == 0:
                    act.wait_ge(bi_done, i + 1)
                act.wait_ge(s1_half, 2 * i + (half + 1))
                need(act, hlo_half, 2 * i + (half - 1))
                for c in range(half * KI // 2, (half + 1) * KI // 2):
                    ins = nc.scalar.activation(h[:, c, :], p_h[parity][:, c, :], ACT.Gelu,
                                               bias=bi_tile[:, parity, c:c + 1], scale=1.0 / (XS * WS))
                ins.then_inc(gelu_half, 1)

            def high_h(i, parity, half):
                cols = slice(half * KI // 2, (half + 1) * KI // 2)
                act.wait_ge(gelu_half, 2 * i + (half + 1))
                nc.scalar.activation(h_hi[:, parity, cols, :], h[:, cols, :], ACT.Copy, scale=HS).then_inc(hhi_half, 1)

            def step(i, parity, weights):
                if exists(i - 3):
                    need(act, a2_done, 2 * i - 6)
                    for n in range(2):
                        d = index(act, 2 * i + (IDX_DOM + n - 6), ENTRIES - 1)
                        nc.scalar.copy(ada_tile[HALF[n], n, :], ada[HALF[n], bass.ds(d, 1), :]).then_inc(ada_done, 1)
                    act.wait_ge(down_done, i - 2)
                    for n in range(2):
                        half = HALF[n]
                        nc.scalar.activation(a1[half, :], p_d[half, S * n:S * n + S], ACT.Gelu,
                                             bias=downb[half, :]).then_inc(a1_done, 1)
                if exists(i):
                    gelu(i, parity, 0)
                    high_h(i, parity, 0)
                if weights:
                    act.wait_ge(w_in[weights[2]], w_loads(i, weights[2]))
                    chunk_high(*weights).then_inc(w_hi, 1)
                if exists(i):
                    gelu(i, parity, 1)
                if exists(i - 2):
                    act.wait_ge(tr_done, i - 1)
                    act.wait_ge(gb_done, i - 1)
                    for k in range(KD):
                        ins = nc.scalar.activation(yT[:, k, :], p_t[:, k * P:k * P + P], ACT.Identity,
                                                   bias=gb_tile[:, KD + k:KD + k + 1], scale=gb_tile[:, k:k + 1])
                    ins.then_inc(yT_done, 1)
                if exists(i):
                    high_h(i, parity, 1)

            act.wait_ge(idx_ready, ALL_READY)
            act.wait_ge(ada_ready, 1)
            act.wait_ge(adapter_in, 8 * 16)
            run(act, step, NCH)

        @block.vector
        def _(dve):
            n_sort = [0]

            def link(ins):
                n_sort[0] += 1
                ins.then_inc(sort_step, 1)
                dve.wait_ge(sort_step, n_sort[0])

            v = nc.vector

            def wide(a):
                return a.unsqueeze(2).to_broadcast([a.shape[0], a.shape[1], E0])

            def rows(a, n):
                return a.unsqueeze(1).to_broadcast([a.shape[0], n, a.shape[1]])

            dve.wait_ge(tok_in, 32)
            dve.wait_ge(iota_ready, 7)
            link(v.tensor_copy(tok[:, :], tok_i[:, :]))
            link(v.tensor_scalar(tmp[:, 0:1], tok[:, 0:1], 0.0, float(E0), ALU.is_lt, ALU.mult))
            link(v.tensor_tensor(tmp[:, 1:2], tok[:, 0:1], tmp[:, 0:1], ALU.add))
            link(v.tensor_scalar(tok[:, 0:1], tmp[:, 1:2], 0.0, float(E0 - 1), ALU.max, ALU.min))
            link(v.tensor_scalar(tmp[:, 2:3], tok[:, 1:2], -1.0, float(E1), ALU.max, ALU.min))
            link(v.tensor_scalar(tmp[:, 0:1], tmp[:, 2:3], 0.0, float(E1 + 1), ALU.is_lt, ALU.mult))
            link(v.tensor_scalar(tmp[:, 1:2], tmp[:, 2:3], float(E1), None, ALU.is_ge))
            link(v.tensor_tensor(tmp[:, 3:4], tmp[:, 2:3], tmp[:, 0:1], ALU.add))
            link(v.tensor_tensor(iota_p[:, 2:3], tmp[:, 3:4], tmp[:, 1:2], ALU.add))
            link(v.tensor_scalar(ident[:, :], below[:, :], 0.0, None, ALU.is_equal))
            link(v.tensor_scalar(below[:, :], below[:, :], 0.0, None, ALU.is_gt))
            link(v.tensor_scalar(lower_e[:, :, :], lower_e[:, :, :], 0.0, None, ALU.is_gt))
            v.tensor_scalar(onehot[:, :], iota_e[:, :], tok[:, 0:1], None, ALU.is_equal).then_inc(counts_ready, 1)
            dve.wait_ge(counts_ready, 2)
            link(v.tensor_scalar(pairs_i[:, :], p_o[:, E0:2 * E0], 1.0, None, ALU.add))
            link(v.tensor_scalar(pairs_h[:, :], pairs_i[:, :], 1, None, ALU.logical_shift_right))
            link(v.tensor_copy(pairs[:, :], pairs_h[:, :]))
            link(v.tensor_tensor(ahead[:, :, :], rows(pairs[:, :], E0), wide(pairs[:, :]), ALU.is_gt))
            link(v.tensor_tensor(same[:, :, :], rows(pairs[:, :], E0), wide(pairs[:, :]), ALU.is_equal))
            link(v.tensor_tensor(same[:, :, :], same[:, :, :], lower_e[:, :, :], ALU.mult))
            link(v.tensor_tensor(ahead[:, :, :], ahead[:, :, :], same[:, :, :], ALU.add))
            link(v.tensor_reduce(place[:, :], ahead[:, :, :], AX.X, ALU.add))
            link(v.tensor_tensor(same[:, :, :], ahead[:, :, :], rows(pairs[:, :], E0), ALU.mult))
            link(v.tensor_reduce(first[:, :], same[:, :, :], AX.X, ALU.add))
            link(v.tensor_tensor(last[:, :], first[:, :], pairs[:, :], ALU.add))
            link(v.scalar_tensor_tensor(where[:, :], first[:, :], 2.0, p_o[:, 0:E0], ALU.mult, ALU.add))
            link(v.tensor_tensor(where[:, :], where[:, :], onehot[:, :], ALU.mult))
            link(v.tensor_reduce(slot[:, :], where[:, :], AX.X, ALU.add))
            link(v.tensor_scalar(at_slot[:, :], iota_r[:, :], slot[:, :], None, ALU.is_equal))
            v.tensor_scalar(before[:, :], iota_r[:, :], slot[:, :], None, ALU.is_gt).then_inc(slots_ready, 1)
            link(v.tensor_tensor(cube[:, 0:E0, :], rows(place[0:1, :], E0), wide(iota_r[0:1, 0:E0]), ALU.is_equal))
            link(v.tensor_tensor(cube[:, 0:E0, :], cube[:, 0:E0, :], rows(iota_e[0:1, :], E0), ALU.mult))
            link(v.tensor_reduce(ord_f[:, :], cube[:, 0:E0, :], AX.X, ALU.add))
            link(v.scalar_tensor_tensor(chunk_f[:, :, :], wide(ord_f[:, :]), float(NCH), rows(iota_e[0:1, :], E0),
                                        ALU.mult, ALU.add))
            v.tensor_copy(idx[:, IDX_CHUNK:IDX_LEN], chunk_f[:, :, :].rearrange("a e c -> a (e c)"))\
                .then_inc(idx_ready, 1)
            dve.wait_ge(rows_ready, 1)
            v.tensor_copy(idx[:, IDX_SRC:IDX_DST], p_t[0:1, 0:SLOTS]).then_inc(idx_ready, 1)
            link(v.tensor_tensor(cube[:, :, :], rows(last[0:1, :], TILES), wide(iota_r[0:1, 0:TILES]), ALU.is_le))
            link(v.tensor_reduce(pos_f[:, :], cube[:, :, :], AX.X, ALU.add))
            link(v.tensor_scalar(pos_f[:, :], pos_f[:, :], float(E0 - 1), None, ALU.min))
            v.tensor_scalar(idx[:, IDX_POS:IDX_EXP], pos_f[:, :], float(PLACE), None, ALU.mult).then_inc(idx_ready, 1)

            def sort_rest():
                link(v.tensor_tensor(cube[:, :, :], rows(place[0:1, :], TILES), wide(pos_f[:, :]), ALU.is_equal))
                link(v.tensor_tensor(cube[:, :, :], cube[:, :, :], rows(iota_e[0:1, :], TILES), ALU.mult))
                link(v.tensor_reduce(exp_f[:, :], cube[:, :, :], AX.X, ALU.add))
                link(v.tensor_copy(idx[:, IDX_EXP:IDX_CHUNK], exp_f[:, :]))
                link(v.tensor_copy(idx[:, IDX_DOM:IDX_POS], p_d[0:1, 0:SLOTS]))
                link(v.tensor_tensor(row[:, 0, :], iota_r[0:1, :], p_u[0:1, 0:SLOTS], ALU.subtract))
                link(v.tensor_scalar(row[:, 1, :], p_o[0:1, 0:SLOTS], -1.0, 1.0, ALU.mult, ALU.add))
                link(v.scalar_tensor_tensor(row[:, 2, :], row[:, 0, :], float(B), row[:, 1, :], ALU.add, ALU.mult))
                link(v.tensor_tensor(row[:, 3, :], row[:, 2, :], p_t[0:1, 0:SLOTS], ALU.add))
                v.tensor_copy(idx[:, IDX_DST:IDX_DOM], row[:, 3, :]).then_inc(idx_ready, 1)

            def high_x(i, parity):
                dve.wait_ge(xT_in[parity], loads(i, parity, 2))
                v.tensor_scalar(x_hi[:, parity, :, :], x_T[:, parity, :, :], XS, None, ALU.mult).then_inc(xhi_done, 1)

            def low_x(i, parity):
                dve.wait_ge(xhi_done, i + 1)
                v.scalar_tensor_tensor(x_lo[:, parity, :, :], x_T[:, parity, :, :], XS, x_hi[:, parity, :, :],
                                       ALU.mult, ALU.subtract).then_inc(x_split, 1)

            def chunk_low(c, place_n, slot_n):
                return v.scalar_tensor_tensor(W[c][:, bass.ds(place_n, 1), :, 1, :],
                                              stage[:, slot_n, :].rearrange("p (a u q) -> p a u q", a=1, u=2),
                                              WS, W[c][:, bass.ds(place_n, 1), :, 0, :], ALU.mult, ALU.subtract)

            for m in range(FIRST_CHUNKS):
                dve.wait_ge(w_first_hi, m + 1)
                chunk_low(m % NCH, m // NCH, m % STAGES).then_inc(w_first, 1)
                if m == NCH // 2 - 1:
                    for i in range(2):
                        high_x(i, i)
                        low_x(i, i)
                    sort_rest()

            def split_h(i, parity, half):
                cols = slice(half * KI // 2, (half + 1) * KI // 2)
                dve.wait_ge(hhi_half, 2 * i + (half + 1))
                v.scalar_tensor_tensor(h_lo[:, parity, cols, :], h[:, cols, :], HS, h_hi[:, parity, cols, :],
                                       ALU.mult, ALU.subtract).then_inc(hlo_half, 1)

            def step(i, parity, weights):
                if exists(i - 2):
                    dve.wait_ge(s2_done, i - 1)
                    dve.wait_ge(xbo_done, i - 1)
                    v.scalar_tensor_tensor(r1[:, :], p_o[:, 0:D], 1.0 / (HS * WS), x_bo[:, parity, :],
                                           ALU.mult, ALU.add).then_inc(r1_done, 1)
                    dve.wait_ge(r1_done, i - 1)
                    v.bn_stats(st1[:, :], r1[:, :]).then_inc(st1_done, 1)
                if exists(i - 2):
                    dve.wait_ge(st1_done, i - 1)
                split_x = exists(i + 1) and not (isinstance(i, int) and i == 0)
                if split_x:
                    high_x(i + 1, 1 - parity)
                if exists(i - 2):
                    v.bn_aggr(mv1[:, :], st1[:, :]).then_inc(mv1_done, 1)
                if exists(i - 3):
                    dve.wait_ge(exp_done, i - 2)
                    for n in range(2):
                        half = HALF[n]
                        v.tensor_scalar(a2[half, S * n:S * n + S], p_d[half, P:P + S], ada_tile[half, n, COL[n]],
                                        None, ALU.add).then_inc(a2_done, 1)
                if exists(i - 2):
                    dve.wait_ge(rs1_done, i - 1)
                    v.tensor_scalar(z1[:, :], r1[:, :], mv1[:, 0:1], rs1[:, :], ALU.subtract, ALU.mult)\
                        .then_inc(z1_done, 1)
                if exists(i):
                    split_h(i, parity, 0)
                if exists(i - 3):
                    dve.wait_ge(up_done, i - 2)
                    dve.wait_ge(yup_done, i - 2)
                    v.tensor_tensor(r2[:, :], p_u[:, 0:D], y_up[:, 1 - parity, :], ALU.add).then_inc(r2_done, 1)
                    dve.wait_ge(r2_done, i - 2)
                    v.bn_stats(st2[:, :], r2[:, :]).then_inc(st2_done, 1)
                if exists(i - 3):
                    dve.wait_ge(st2_done, i - 2)
                if split_x:
                    low_x(i + 1, 1 - parity)
                if exists(i - 3):
                    v.bn_aggr(mv2[:, :], st2[:, :]).then_inc(mv2_done, 1)
                if weights:
                    dve.wait_ge(w_hi, i + 1)
                    chunk_low(*weights).then_inc(w_lo, 1)
                if exists(i):
                    split_h(i, parity, 1)
                if exists(i - 3):
                    dve.wait_ge(rs2_done, i - 2)
                    v.tensor_scalar(z2[:, :], r2[:, :], mv2[:, 0:1], rs2[:, :], ALU.subtract, ALU.mult)\
                        .then_inc(z2_done, 1)

            run(dve, step, NCH)

        @block.tensor
        def _(pe):
            mm = nc.tensor.matmul
            DOWN_AT, EXP_AT, UP_AT, TR_AT = 1, 5, 9, 2
            pe.wait_ge(counts_ready, 1)
            pe.wait_ge(iota_ready, 7)
            mm(p_o[:, 0:E0], below[:, :], onehot[:, :], start=True, stop=True)
            mm(p_o[:, E0:2 * E0], ones[:, :], onehot[:, :], start=True, stop=True).then_inc(counts_ready, 1)
            pe.wait_ge(slots_ready, 1)
            mm(p_t[0:1, 0:SLOTS], iota_p[:, 0:1], at_slot[:, :], start=True, stop=True)
            mm(p_o[0:1, 0:SLOTS], iota_p[:, 1:2], at_slot[:, :], start=True, stop=True)
            mm(p_d[0:1, 0:SLOTS], iota_p[:, 2:3], at_slot[:, :], start=True, stop=True)
            mm(p_u[0:1, 0:SLOTS], iota_p[:, 1:2], before[:, :], start=True, stop=True).then_inc(rows_ready, 1)
            pe.wait_ge(idx_ready, TILE_READY)
            pe.wait_ge(const_ready, 5)

            def first_weights(place_reg, c, k):
                chunk, at = w_flat[k * 2 + c // 4], c % 4 // 2 * WCH + c % 2 * P
                return chunk[:, bass.ds(place_reg + at, P)], chunk[:, bass.ds(place_reg + (at + QC), P)]

            def second_weights(place_reg, j):
                chunk, at = w_flat[NCH // 2 + j // 2], j % 2 * WCH
                return chunk[:, bass.ds(place_reg + at, D)], chunk[:, bass.ds(place_reg + (at + D), D)]

            def first_addresses(place_reg, cs):
                for k in range(KD):
                    for c in cs:
                        for part in first_weights(place_reg, c, k):
                            pe.lower_ap(part, for_matmul_weights=True)

            def second_addresses(place_reg, js):
                for j in js:
                    for part in second_weights(place_reg, j):
                        pe.lower_ap(part)

            def first_product(parity, place_reg, c):
                for k in range(KD):
                    hi, lo = first_weights(place_reg, c, k)
                    mm(p_h[parity][:, c, :], hi, x_hi[:, parity, k, :], start=(k == 0), stop=False)
                    mm(p_h[parity][:, c, :], hi, x_lo[:, parity, k, :], start=False, stop=False)
                    ins = mm(p_h[parity][:, c, :], lo, x_hi[:, parity, k, :], start=False, stop=(k == KD - 1))
                return ins

            def second_product(parity, place_reg, j):
                hi, lo = second_weights(place_reg, j)
                mm(p_o[:, 0:D], h_hi[:, parity, j, :], hi, start=(j == 0), stop=False)
                mm(p_o[:, 0:D], h_hi[:, parity, j, :], lo, start=False, stop=False)
                return mm(p_o[:, 0:D], h_lo[:, parity, j, :], hi, start=False, stop=(j == KI - 1))

            def step(i, parity, weights):
                def down():
                    pe.wait_ge(yT_done, i - 2)
                    for k in range(KD):
                        ins = mm(p_d[:, 0:P], downT[:, k, :, :], yT[:, k, :], start=(k == 0), stop=(k == KD - 1))
                    ins.then_inc(down_done, 1)

                def expert():
                    pe.wait_ge(a1_done, 2 * i - 4)
                    mm(p_d[:, P:P + S], ada_tile[:, :, :].rearrange("p n a -> p (n a)")[:, 1:2 * A + 1], a1[:, :],
                       start=True, stop=True).then_inc(exp_done, 1)

                def up():
                    pe.wait_ge(a2_done, 2 * i - 4)
                    mm(p_u[:, 0:D], a2[:, :], upT[:, :], start=True, stop=True).then_inc(up_done, 1)

                def transpose():
                    pe.wait_ge(z1_done, i - 1)
                    for k in range(KD):
                        ins = nc.tensor.transpose(p_t[:, k * P:k * P + P], z1[:, k * P:k * P + P], ident[:, :])
                    ins.then_inc(tr_done, 1)

                between = {DOWN_AT: down, EXP_AT: expert, UP_AT: up} if exists(i - 3) else {}
                if exists(i):
                    here = index(pe, i + IDX_POS, (E0 - 1) * PLACE)
                    first_addresses(here, range(2))
                    pe.wait_ge(x_split, i + 1)
                    if isinstance(i, int) and i == 0:
                        pe.wait_ge(w_first, NCH // 2)
                for c in range(KI):
                    if exists(i):
                        if c in (1, 3, 5):
                            first_addresses(here, range(c + 1, c + 3))
                        ins = first_product(parity, here, c)
                        if c % (KI // 2) == KI // 2 - 1:
                            ins.then_inc(s1_half, 1)
                    if exists(i - 1):
                        if c == 0:
                            there = index(pe, i + (IDX_POS - 1), (E0 - 1) * PLACE)
                        if c in (2, 4):
                            second_addresses(there, range(2 * c - 4, 2 * c))
                    if c in between:
                        between[c]()
                if exists(i - 1):
                    if isinstance(i, int) and i == 1:
                        pe.wait_ge(w_first, FIRST_CHUNKS)
                    elif weights:
                        pe.wait_ge(w_lo, i - 1)
                    else:
                        pe.wait_ge(w_lo, CHUNKS - FIRST_CHUNKS)
                    pe.wait_ge(hlo_half, 2 * i)
                    need(pe, r1_done, i - 1)
                for j in range(KI):
                    if j + KI in between:
                        between[j + KI]()
                    if j == TR_AT and exists(i - 2):
                        transpose()
                    if exists(i - 1):
                        ins = second_product(1 - parity, there, j)
                        if j == KI - 1:
                            ins.then_inc(s2_done, 1)

            pe.wait_ge(adapter_in, 8 * 16)
            run(pe, step)


def kernel(x, itok_B_0_7, itok_B_0_15, L0_cond_Wi, L0_cond_bi, L0_cond_Wo, L0_cond_bo, L0_cond_gamma,
           L0_cond_beta, L1_cond_down_W, L1_cond_down_b, L1_cond_up_W, L1_cond_up_b, L1_cond_expert_W,
           L1_cond_expert_b, L1_cond_domain_emb, L1_cond_ln_gamma, L1_cond_ln_beta):
    import numpy as np
    import concourse.bacc as bacc
    from concourse.bass_utils import run_bass_kernel_spmd

    wi = np.asarray(L0_cond_Wi).reshape(E0, KD, P, I // WCH, WCH).transpose(0, 1, 3, 2, 4)
    wo = np.asarray(L0_cond_Wo).reshape(E0, NCH // 2, WCH // D, P, D).transpose(0, 1, 3, 2, 4)
    w = np.concatenate([wi.reshape(E0, NCH // 2, P, WCH), wo.reshape(E0, NCH // 2, P, WCH)], axis=1)
    g = np.asarray(L0_cond_gamma).reshape(E0, KD, P).transpose(2, 0, 1)
    be = np.asarray(L0_cond_beta).reshape(E0, KD, P).transpose(2, 0, 1)
    arrays = {
        "itok0": itok_B_0_7,
        "itok1": itok_B_0_15,
        "x": np.asarray(x).reshape(B * S, D),
        "xT": np.asarray(x).reshape(B, S, KD, P).transpose(0, 3, 2, 1).reshape(B * P, KD * S),
        "w": w.reshape(CHUNKS * P, WCH),
        "bi": np.asarray(L0_cond_bi).reshape(E0, KI, P).transpose(2, 0, 1).reshape(P, E0 * KI),
        "gb": np.concatenate([g, be], axis=2).reshape(P, E0 * 2 * KD),
        "bo": np.asarray(L0_cond_bo).reshape(E0 * D),
        "gamma": np.asarray(L0_cond_gamma).reshape(E0 * D),
        "beta": np.asarray(L0_cond_beta).reshape(E0 * D),
        "down_W": np.asarray(L1_cond_down_W).T,
        "down_b": L1_cond_down_b,
        "up_W": np.asarray(L1_cond_up_W).T,
        "up_b": L1_cond_up_b,
        "expert_W": np.asarray(L1_cond_expert_W).transpose(2, 0, 1),
        "expert_b": np.asarray(L1_cond_expert_b).T,
        "emb": np.asarray(L1_cond_domain_emb).T,
        "ln_gamma": L1_cond_ln_gamma,
        "ln_beta": L1_cond_ln_beta,
    }
    nc = bacc.Bacc("TRN2", target_bir_lowering=False, num_devices=1)
    fed, t = {}, {}
    for name, a in arrays.items():
        a = np.ascontiguousarray(a)
        fed[f"in_{name}"] = a
        t[name] = nc.dram_tensor(f"in_{name}", a.shape, mybir.dt.from_np(a.dtype), kind="ExternalInput").ap()
    t["out"] = nc.dram_tensor("out", (SLOTS * S, D), mybir.dt.float32, kind="ExternalOutput").ap()
    build(nc, t)
    got = run_bass_kernel_spmd(nc, [fed], core_ids=[0]).results[0]["out"]
    return got.reshape(SLOTS, S, D)[:B]
```
